# Optimizing a Trainium2 kernel written in Bass

```python
import numpy as np
import jax
import jax.numpy as jnp

def _softmax(x, axis=-1):
    return jax.nn.softmax(x, axis=axis)

def _gelu(x):
    return jax.nn.gelu(x, approximate=True)

def _silu(x):
    return jax.nn.silu(x)

def _sigmoid(x):
    return jax.nn.sigmoid(x)

def _layernorm(x, axis=-1, eps=1e-05):
    m = jnp.mean(x, axis=axis, keepdims=True)
    v = jnp.var(x, axis=axis, keepdims=True)
    return (x - m) / jnp.sqrt(v + eps)

def _scatter_add(tgt, idx, src, axis=0):
    return tgt.at[idx].add(src)

def _segment_sum(src, seg, n):
    return jax.ops.segment_sum(src, seg, n)
kernel_name = 'mk_seq_postln_d1_jaxref_r8_fe4c9a'

def setup_inputs(seed: int=0):
    np.random.seed(seed)
    _w = jnp.asarray

    def _L0_attn_setup():
        import jax, jax.numpy as jnp
        import numpy as np
        LAYERS, DIM, FFN, HEADS = (2, 128, 512, 8)
        HD = DIM // HEADS
        VD = DIM
        HV = VD // HEADS
        B, L = (2, 256)
        SCALE_BASE = 512.0
        EPS = 1e-05

        def _xpos_tables(length, head_dim):
            half = head_dim // 2
            pos = jnp.arange(length, dtype=jnp.float32)
            base_scale = (jnp.arange(0, head_dim, 2, dtype=jnp.float32) + 0.4 * head_dim) / (1.4 * head_dim)
            sc = base_scale[None, :] ** (pos / SCALE_BASE)[:, None]
            inv_freq = 1.0 / 10000.0 ** (jnp.arange(half, dtype=jnp.float32) / half)
            ang = pos[:, None] * inv_freq[None, :]
            return (sc, jnp.sin(ang), jnp.cos(ang))

        def _dup(t):
            return jnp.repeat(t, 2, axis=-1)

        def _rotate_every_two(x):
            x1, x2 = (x[..., ::2], x[..., 1::2])
            return jnp.stack([-x2, x1], axis=-1).reshape(x.shape)

        def _apply_xpos(x, sc, sin, cos, downscale):
            s = 1.0 / sc if downscale else sc
            return x * _dup(cos * s) + _rotate_every_two(x) * _dup(sin * s)

        def _layernorm(x, w, b):
            mu = jnp.mean(x, axis=-1, keepdims=True)
            var = jnp.var(x, axis=-1, keepdims=True)
            return (x - mu) * jax.lax.rsqrt(var + EPS) * w + b

        def _decay_matrix(length):
            gammas = jnp.asarray(1.0 - np.exp(np.linspace(np.log(1 / 32), np.log(1 / 64), HEADS)), dtype=jnp.float32)
            n = jnp.arange(length, dtype=jnp.float32)
            delta = n[:, None] - n[None, :]
            logg = jnp.log(gammas)[:, None, None]
            return jnp.where(delta[None] >= 0, jnp.exp(logg * delta[None]), 0.0)

        def _msr(X, Wq, Wk, Wv, gn_w, gn_b, W_G, W_O, D, sc, sin, cos):
            b, l, d = X.shape
            Q = _apply_xpos(jnp.einsum('bld,hde->bhle', X, Wq), sc, sin, cos, False)
            K = _apply_xpos(jnp.einsum('bld,hde->bhle', X, Wk), sc, sin, cos, True)
            V = jnp.einsum('bld,hdv->bhlv', X, Wv)
            scores = jnp.einsum('bhle,bhme->bhlm', Q, K) * D[None]
            Y = jnp.einsum('bhlm,bhmv->bhlv', scores, V)
            mu = jnp.mean(Y, axis=-1, keepdims=True)
            var = jnp.var(Y, axis=-1, keepdims=True)
            Yn = (Y - mu) * jax.lax.rsqrt(var + EPS)
            Yn = Yn * gn_w.reshape(HEADS, 1, HV)[None] + gn_b.reshape(HEADS, 1, HV)[None]
            Yc = jnp.transpose(Yn, (0, 2, 1, 3)).reshape(b, l, VD)
            G = X @ W_G
            gate = G * jax.nn.sigmoid(G)
            return gate * Yc @ W_O
        key = jax.random.key(seed)
        ks = jax.random.split(key, 18)

        def rn(k, shape, s=1.0):
            return jax.random.normal(k, shape, dtype=jnp.float32) * s
        return dict(X=rn(ks[0], (B, L, DIM)), Wq=rn(ks[1], (LAYERS, HEADS, DIM, HD), 1.0 / DIM), Wk=rn(ks[2], (LAYERS, HEADS, DIM, HD), 1.0 / DIM), Wv=rn(ks[3], (LAYERS, HEADS, DIM, HV), 1.0 / DIM), W_G=rn(ks[4], (LAYERS, DIM, VD), 1.0 / DIM), W_O=rn(ks[5], (LAYERS, VD, DIM), 1.0 / DIM), gn_w=1.0 + 0.02 * rn(ks[6], (LAYERS, VD)), gn_b=0.02 * rn(ks[7], (LAYERS, VD)), ln1_w=1.0 + 0.02 * rn(ks[8], (LAYERS, DIM)), ln1_b=0.02 * rn(ks[9], (LAYERS, DIM)), ln2_w=1.0 + 0.02 * rn(ks[10], (LAYERS, DIM)), ln2_b=0.02 * rn(ks[11], (LAYERS, DIM)), ffn_w1=rn(ks[12], (LAYERS, DIM, FFN), DIM ** (-0.5)), ffn_b1=0.02 * rn(ks[13], (LAYERS, FFN)), ffn_w2=rn(ks[14], (LAYERS, FFN, DIM), FFN ** (-0.5)), ffn_b2=0.02 * rn(ks[15], (LAYERS, DIM)))
    _L0_attn_in = _L0_attn_setup()

    def _L0_ffn_setup():
        import jax, jax.numpy as jnp
        import numpy as np
        H = 32
        MB = 2
        TOP_K = 2
        key = jax.random.key(seed)
        ks = jax.random.split(key, 8)
        B, S, D, E = (8, 128, 128, 8)
        Fd = 4 * D

        def w(k, shape, fan):
            return jax.random.normal(k, shape, jnp.float32) / np.float32(np.sqrt(fan))
        return dict(x=jax.random.normal(ks[0], (B, S, D), jnp.float32), ln_g=jnp.ones((D,), jnp.float32), ln_b=jnp.zeros((D,), jnp.float32), wq=w(ks[1], (D, D), D), wk=w(ks[2], (D, D), D), wv=w(ks[3], (D, D), D), wo=w(ks[4], (D, D), D), gate_w=w(ks[5], (E, D), D), w1=w(ks[6], (E, D, Fd), D), b1=jnp.zeros((E, Fd), jnp.float32), w2=w(ks[7], (E, Fd, D), Fd), b2=jnp.zeros((E, D), jnp.float32))
    _L0_ffn_in = _L0_ffn_setup()
    _d = {'L0_attn_X': _L0_attn_in['X'], 'L0_attn_Wq': _L0_attn_in['Wq'], 'L0_attn_Wk': _L0_attn_in['Wk'], 'L0_attn_Wv': _L0_attn_in['Wv'], 'L0_attn_W_G': _L0_attn_in['W_G'], 'L0_attn_W_O': _L0_attn_in['W_O'], 'L0_attn_gn_w': _L0_attn_in['gn_w'], 'L0_attn_gn_b': _L0_attn_in['gn_b'], 'L0_attn_ln1_w': _L0_attn_in['ln1_w'], 'L0_attn_ln1_b': _L0_attn_in['ln1_b'], 'L0_attn_ln2_w': _L0_attn_in['ln2_w'], 'L0_attn_ln2_b': _L0_attn_in['ln2_b'], 'L0_attn_ffn_w1': _L0_attn_in['ffn_w1'], 'L0_attn_ffn_b1': _L0_attn_in['ffn_b1'], 'L0_attn_ffn_w2': _L0_attn_in['ffn_w2'], 'L0_attn_ffn_b2': _L0_attn_in['ffn_b2'], 'L0_ffn_ln_g': _L0_ffn_in['ln_g'], 'L0_ffn_ln_b': _L0_ffn_in['ln_b'], 'L0_ffn_wq': _L0_ffn_in['wq'], 'L0_ffn_wk': _L0_ffn_in['wk'], 'L0_ffn_wv': _L0_ffn_in['wv'], 'L0_ffn_wo': _L0_ffn_in['wo'], 'L0_ffn_gate_w': _L0_ffn_in['gate_w'], 'L0_ffn_w1': _L0_ffn_in['w1'], 'L0_ffn_b1': _L0_ffn_in['b1'], 'L0_ffn_w2': _L0_ffn_in['w2'], 'L0_ffn_b2': _L0_ffn_in['b2']}
    _x0 = _d['L0_attn_X']
    _d['L0_attn_X'] = jax.random.normal(jax.random.fold_in(jax.random.key(seed), 1), (32, 256, 128), dtype=_x0.dtype)
    del _x0
    return _d

def reference(L0_attn_X, L0_attn_Wq, L0_attn_Wk, L0_attn_Wv, L0_attn_W_G, L0_attn_W_O, L0_attn_gn_w, L0_attn_gn_b, L0_attn_ln1_w, L0_attn_ln1_b, L0_attn_ln2_w, L0_attn_ln2_b, L0_attn_ffn_w1, L0_attn_ffn_b1, L0_attn_ffn_w2, L0_attn_ffn_b2, L0_ffn_ln_g, L0_ffn_ln_b, L0_ffn_wq, L0_ffn_wk, L0_ffn_wv, L0_ffn_wo, L0_ffn_gate_w, L0_ffn_w1, L0_ffn_b1, L0_ffn_w2, L0_ffn_b2):

    def _L0_attn_ref(X, Wq, Wk, Wv, W_G, W_O, gn_w, gn_b, ln1_w, ln1_b, ln2_w, ln2_b, ffn_w1, ffn_b1, ffn_w2, ffn_b2):
        import jax, jax.numpy as jnp
        import numpy as np
        LAYERS, DIM, FFN, HEADS = (2, 128, 512, 8)
        HD = DIM // HEADS
        VD = DIM
        HV = VD // HEADS
        B, L = (2, 256)
        SCALE_BASE = 512.0
        EPS = 1e-05

        def _xpos_tables(length, head_dim):
            half = head_dim // 2
            pos = jnp.arange(length, dtype=jnp.float32)
            base_scale = (jnp.arange(0, head_dim, 2, dtype=jnp.float32) + 0.4 * head_dim) / (1.4 * head_dim)
            sc = base_scale[None, :] ** (pos / SCALE_BASE)[:, None]
            inv_freq = 1.0 / 10000.0 ** (jnp.arange(half, dtype=jnp.float32) / half)
            ang = pos[:, None] * inv_freq[None, :]
            return (sc, jnp.sin(ang), jnp.cos(ang))

        def _dup(t):
            return jnp.repeat(t, 2, axis=-1)

        def _rotate_every_two(x):
            x1, x2 = (x[..., ::2], x[..., 1::2])
            return jnp.stack([-x2, x1], axis=-1).reshape(x.shape)

        def _apply_xpos(x, sc, sin, cos, downscale):
            s = 1.0 / sc if downscale else sc
            return x * _dup(cos * s) + _rotate_every_two(x) * _dup(sin * s)

        def _layernorm(x, w, b):
            mu = jnp.mean(x, axis=-1, keepdims=True)
            var = jnp.var(x, axis=-1, keepdims=True)
            return (x - mu) * jax.lax.rsqrt(var + EPS) * w + b

        def _decay_matrix(length):
            gammas = jnp.asarray(1.0 - np.exp(np.linspace(np.log(1 / 32), np.log(1 / 64), HEADS)), dtype=jnp.float32)
            n = jnp.arange(length, dtype=jnp.float32)
            delta = n[:, None] - n[None, :]
            logg = jnp.log(gammas)[:, None, None]
            return jnp.where(delta[None] >= 0, jnp.exp(logg * delta[None]), 0.0)

        def _msr(X, Wq, Wk, Wv, gn_w, gn_b, W_G, W_O, D, sc, sin, cos):
            b, l, d = X.shape
            Q = _apply_xpos(jnp.einsum('bld,hde->bhle', X, Wq), sc, sin, cos, False)
            K = _apply_xpos(jnp.einsum('bld,hde->bhle', X, Wk), sc, sin, cos, True)
            V = jnp.einsum('bld,hdv->bhlv', X, Wv)
            scores = jnp.einsum('bhle,bhme->bhlm', Q, K) * D[None]
            Y = jnp.einsum('bhlm,bhmv->bhlv', scores, V)
            mu = jnp.mean(Y, axis=-1, keepdims=True)
            var = jnp.var(Y, axis=-1, keepdims=True)
            Yn = (Y - mu) * jax.lax.rsqrt(var + EPS)
            Yn = Yn * gn_w.reshape(HEADS, 1, HV)[None] + gn_b.reshape(HEADS, 1, HV)[None]
            Yc = jnp.transpose(Yn, (0, 2, 1, 3)).reshape(b, l, VD)
            G = X @ W_G
            gate = G * jax.nn.sigmoid(G)
            return gate * Yc @ W_O
        l = X.shape[1]
        sc, sin, cos = _xpos_tables(l, HD)
        D = _decay_matrix(l)
        for i in range(LAYERS):
            Y = _msr(_layernorm(X, ln1_w[i], ln1_b[i]), Wq[i], Wk[i], Wv[i], gn_w[i], gn_b[i], W_G[i], W_O[i], D, sc, sin, cos) + X
            h = _layernorm(Y, ln2_w[i], ln2_b[i])
            h = jax.nn.gelu(h @ ffn_w1[i] + ffn_b1[i], approximate=False)
            X = h @ ffn_w2[i] + ffn_b2[i] + Y
        return X

    def _L0_ffn_ref(x, ln_g, ln_b, wq, wk, wv, wo, gate_w, w1, b1, w2, b2):
        import jax, jax.numpy as jnp
        import numpy as np
        H = 32
        MB = 2
        TOP_K = 2
        B, S, D = x.shape
        E = w1.shape[0]
        hd = D // H
        mu = jnp.mean(x, axis=-1, keepdims=True)
        var = jnp.var(x, axis=-1, keepdims=True)
        xn = (x - mu) / jnp.sqrt(var + 1e-05) * ln_g + ln_b
        q = (xn @ wq).reshape(B, S, H, hd)
        k = (xn @ wk).reshape(B, S, H, hd)
        v = (xn @ wv).reshape(B, S, H, hd)
        att = jnp.einsum('bqhd,bkhd->bhqk', q, k) / np.float32(np.sqrt(hd))
        p = jax.nn.softmax(att, axis=-1)
        o = jnp.einsum('bhqk,bkhd->bqhd', p, v).reshape(B, S, D) @ wo + x
        xf = o.reshape(-1, D)
        logits = xf @ gate_w.T
        _ = jax.lax.top_k(logits, TOP_K)
        tpe = xf.shape[0] // (MB * E)
        xe = xf.reshape(MB, E, tpe, D)
        h = jax.nn.gelu(jnp.einsum('metd,edf->metf', xe, w1) + b1[None, :, None, :], approximate=False)
        y = jnp.einsum('metf,efd->metd', h, w2) + b2[None, :, None, :]
        return y.reshape(B, S, D)
    x = L0_attn_X
    x = _layernorm(x + _L0_attn_ref(x, L0_attn_Wq, L0_attn_Wk, L0_attn_Wv, L0_attn_W_G, L0_attn_W_O, L0_attn_gn_w, L0_attn_gn_b, L0_attn_ln1_w, L0_attn_ln1_b, L0_attn_ln2_w, L0_attn_ln2_b, L0_attn_ffn_w1, L0_attn_ffn_b1, L0_attn_ffn_w2, L0_attn_ffn_b2), axis=-1)
    x = _layernorm(x + _L0_ffn_ref(x, L0_ffn_ln_g, L0_ffn_ln_b, L0_ffn_wq, L0_ffn_wk, L0_ffn_wv, L0_ffn_wo, L0_ffn_gate_w, L0_ffn_w1, L0_ffn_b1, L0_ffn_w2, L0_ffn_b2), axis=-1)
    return x

_drawn_inputs = setup_inputs


def setup_inputs(seed=0):
    import zlib

    import numpy as np

    out = dict(_drawn_inputs(seed))
    spreads = {'L0_ffn_ln_g': (1.0, 0.2),
     'L0_ffn_ln_b': (0.0, 0.1),
     'L0_ffn_b1': (0.0, 0.1),
     'L0_ffn_b2': (0.0, 0.1)}
    factors = {'L0_attn_Wq': 8.0,
     'L0_attn_Wk': 8.0,
     'L0_attn_Wv': 8.0,
     'L0_attn_W_G': 8.0,
     'L0_attn_W_O': 8.0,
     'L0_attn_gn_w': 8.0,
     'L0_attn_gn_b': 8.0,
     'L0_attn_ln1_w': 8.0,
     'L0_attn_ln1_b': 8.0,
     'L0_attn_ln2_w': 37.496,
     'L0_attn_ln2_b': 26.858,
     'L0_attn_ffn_b1': 40.341,
     'L0_attn_ffn_b2': 51.815}
    for name, (base, spread) in spreads.items():
        noise = np.random.default_rng([zlib.crc32(name.encode()), seed]).standard_normal(out[name].shape)
        drawn = base * np.exp(spread * noise) if base else spread * noise
        out[name] = jnp.asarray(drawn.astype(out[name].dtype))
    for name, factor in factors.items():
        out[name] = (out[name] * factor).astype(out[name].dtype)
    return out
```

```python
from contextlib import ExitStack

import concourse.bass as bass
from concourse import mybir

F32 = mybir.dt.float32
BF16 = mybir.dt.bfloat16
ALU = mybir.AluOpType
ACT = mybir.ActivationFunctionType
AX = mybir.AxisListType

P = 128
D = 128
FFN = 512
NF = FFN // P
LAYERS = 2
SEQS, L = 32, 256
UNIT = 512
NC = UNIT // P
SPU = UNIT // L
UNITS = SEQS // SPU
TURNS = UNITS // 2
EPS = 1e-5

PARTS = 3
Q_PART = (0, 0, 1, 1, 0, 2)
K_PART = (0, 1, 0, 1, 2, 0)
TERMS = len(Q_PART)

RH, RE = 8, 16
RROWS = TERMS * RE
HEADS = SPU * RH
STACK_DMAS = 2 * TERMS

AH, AE = 32, 4
QUADS = 4
TILES = AH // QUADS
SLOT = 8
EXPERTS = 8
VW = 2 * AE


def flat(t):
    return t.rearrange("p a b -> p (a b)")


def layer_norm_stats(nc, dve, src, bn, mv, halves_done, halves_seen, done, count):
    for c in range(NC):
        last = nc.vector.bn_stats(bn[:, c], src[:, c])
    last.then_inc(halves_done, 1)
    dve.wait_ge(halves_done, count)
    dve.sem_inc(halves_seen, 1)
    for c in range(NC):
        last = nc.vector.bn_aggr(mv[:, c], bn[:, c])
    last.then_inc(done, 1)


def inverse_root(nc, pool, mv, var, rstd, eps, minus_half, stats_done, var_done, done, count):
    pool.wait_ge(stats_done, count)
    nc.gpsimd.tensor_tensor(var[:], mv[:, :, 1], eps[:], ALU.add).then_inc(var_done, 1)
    pool.wait_ge(var_done, count)
    nc.gpsimd.tensor_tensor(rstd[:], var[:], minus_half[:], ALU.pow).then_inc(done, 1)


def normalise(nc, dve, src, dst, mv, rstd, rstd_done, count, done):
    dve.wait_ge(rstd_done, count)
    for c in range(NC):
        last = nc.vector.tensor_scalar(dst[:, c], src[:, c], mv[:, c, 0:1], rstd[:, c:c + 1],
                                       ALU.subtract, ALU.mult)
    last.then_inc(done, 1)


def retention_block(nc, bank, x1_all, X, Wq, Wk, Wv, W_G, W_O, gn_w, gn_b, ln1_w, ln1_b, ln2_w, ln2_b,
                    ffn_w1, ffn_b1, ffn_w2, ffn_b2, c_xpos, c_mask, c_ident):
    x_units = X.rearrange("(n s) (h p) d -> p n (s h) d", s=SPU, p=P)

    with ExitStack() as ctx:
        def sb(name, shape, dt=F32):
            return ctx.enter_context(nc.sbuf_tensor(name, shape, dt))

        def two(name, shape, dt=F32):
            return [sb(f"{name}{u}", shape, dt) for u in range(2)]

        used = []

        def sem(name):
            used.append(nc.alloc_semaphore(name))
            return used[-1]

        def sems(names):
            return [[sem(f"{n}_{u}") for u in range(2)] for n in names.split()]

        ident = sb("ident", [P, P])
        xpos = sb("xpos", [P, 4, L])
        mask = sb("mask", [P, P])
        minus_half = sb("minus_half", [P, NC])
        eps = sb("eps", [P, NC])
        wqk_raw = sb("wqk_raw", [P, LAYERS, 2, RH, RE])
        wqk = sb("wqk", [P, LAYERS, 4, RE, RH])
        wv_s = sb("wv_s", [P, LAYERS, RH, RE])
        wg_s = sb("wg_s", [P, LAYERS, D])
        wo_s = sb("wo_s", [P, LAYERS, D])
        w1_s = sb("w1_s", [P, LAYERS, FFN])
        w2_s = sb("w2_s", [P, LAYERS, NF, D])
        b1_s = sb("b1_s", [P, LAYERS, NF])
        b2_s = sb("b2_s", [P, LAYERS, D])
        gnw_s = sb("gnw_s", [P, LAYERS, D])
        gnb_s = sb("gnb_s", [P, LAYERS, D])
        ln_s = sb("ln_s", [P, 4, LAYERS])

        xin = two("xin", [P, NC, D])
        res = two("res", [P, NC, D])
        resb = two("resb", [P, NC, D])
        bn = two("bn", [P, NC, 6])
        mv = two("mv", [P, NC, 2])
        var = two("var", [P, NC])
        rstd = two("rstd", [P, NC])
        xh = two("xh", [P, NC, D])
        hT = two("hT", [P, UNIT])
        rot_a = two("rot_a", [P, UNIT])
        rot_b = two("rot_b", [P, UNIT])
        qk = two("qk", [P, 2, UNIT])
        part = two("part", [P, 2, PARTS, UNIT], BF16)
        q_stack = two("q_stack", [P, RH, UNIT], BF16)
        k_stack = two("k_stack", [P, RH, UNIT], BF16)
        v_pad = two("v_pad", [P, NC, RH, 2 * RE])
        gate_t = two("gate_t", [P, UNIT])
        gate = two("gate", [P, NC, D])
        gate_w = two("gate_w", [P, NC, D])
        gate_b = two("gate_b", [P, NC, D])
        PB = 4
        prob = [[sb(f"prob{u}{i}", [P, 3, P]) for i in range(PB)] for u in range(2)]
        y = two("y", [P, UNIT])
        g_sum = two("g_sum", [P, NC * RH])
        g_stat = two("g_stat", [P, NC * RH])
        dev = two("dev", [P, NC, D])
        zT = two("zT", [P, UNIT])
        hidden = two("hidden", [P, NF, UNIT])

        stacks_free = sem("stacks_free")
        loaded, turned_w, padded = sem("weights_loaded"), sem("weights_turned"), sem("v_pad_zeroed")
        x_in, x_summed, x1_ready, x1_stored = sems("x_in x_summed x1_ready x1_stored")
        n_half, n_seen, n_stat, n_var, n_root = sems("n_half n_seen n_stat n_var n_root")
        n1_done, n1_turn, n1_hT = sems("n1_done n1_turn n1_hT")
        n2_done, n2_turn, n2_hT = sems("n2_done n2_turn n2_hT")
        q_mm, qt_mm, k_mm, kt_mm, v_mm, g_mm = sems("q_mm qt_mm k_mm kt_mm v_mm g_mm")
        mm_of = ((q_mm, qt_mm), (k_mm, kt_mm))
        rotated, full = sems("q_rotated k_rotated"), sems("q_full k_full")
        part_done = [sems(f"{q}_part0 {q}_part1 {q}_part2") for q in "qk"]
        part_left = sems("q_left k_left")
        stacked, = sems("stacked")
        v_ready, tanh_done, gate_done, gates_done = sems("v_ready tanh_done gate_done gates_done")
        s_mm, s_off, s_masked, pv_mm = sems("s_mm s_off s_masked pv_mm")
        y_done, y_turn = sems("y_done y_turn")
        g_sum_done, g_mean, g_dev, g_sq, g_sqsum, g_var, g_sd, g_root, g_norm, g_scaled, z_done = sems(
            "g_sum_done g_mean g_dev g_sq g_sqsum g_var g_sd g_root g_norm g_scaled z_done")
        z_turn, zT_done, o_mm, o_res, resb_done, f2_mm, f_res = sems(
            "z_turn zT_done o_mm o_res resb_done f2_mm f_res")
        f1_mm = sems("f1_mm0 f1_mm1 f1_mm2 f1_mm3")
        gelu_done = sems("gelu0 gelu1 gelu2 gelu3")

        def B(u, i):
            return bank[4 * u + i]

        def norm_count(it, l, second=0):
            return it * (2 * LAYERS + 1) + (2 * l + second + 1)

        def chunk(t, c):
            return t[:, c * P:(c + 1) * P]

        F_BANK = (2, 3, 0, 1)
        S_BANK = (3, 0)

        loads = [(ident[:], c_ident), (xpos[:], c_xpos), (mask[:], c_mask)]
        for l in range(LAYERS):
            loads += [(wqk_raw[:, l, 0], Wq[l].rearrange("h d e -> d h e")),
                      (wqk_raw[:, l, 1], Wk[l].rearrange("h d e -> d h e")),
                      (wv_s[:, l], Wv[l].rearrange("h d e -> d h e")),
                      (wg_s[:, l], W_G[l]), (wo_s[:, l], W_O[l]), (w1_s[:, l], ffn_w1[l]),
                      (w2_s[:, l], ffn_w2[l].rearrange("(f p) n -> p f n", p=P)),
                      (b1_s[:, l], ffn_b1[l].rearrange("(f p) -> p f", p=P)),
                      (b2_s[:, l], ffn_b2[l:l + 1, :].to_broadcast([P, D])),
                      (gnw_s[:, l], gn_w[l:l + 1, :].to_broadcast([P, D])),
                      (gnb_s[:, l], gn_b[l:l + 1, :].to_broadcast([P, D]))]
            loads += [(ln_s[:, i, l:l + 1], v[l].rearrange("(p a) -> p a", a=1))
                      for i, v in enumerate((ln1_w, ln1_b, ln2_w, ln2_b))]
        all_loaded = 16 * len(loads)

        block = ctx.enter_context(nc.Block())

        @block.sync
        def _(sp):
            for dst, src in loads:
                with nc.allow_non_contiguous_dma("weights, once"):
                    sp.dma_start(dst, src).then_inc(loaded, 16)
            with sp.Fori(0, TURNS) as it:
                turn = sp.snap(it + 1)
                unit = [sp.snap(it * 2 + u) for u in range(2)]
                for u in range(2):
                    sp.wait_ge(x_summed[u], it)
                    sp.dma_start(xin[u][:].unsqueeze(1), x_units[:, bass.ds(unit[u], 1)]
                                 ).then_inc(x_in[u], 16)
                for l in range(LAYERS):
                    n = sp.snap(it * LAYERS + (l + 1))
                    for u in range(2):
                        sp.wait_ge(pv_mm[u], (n - 1) * HEADS)
                        sp.sem_inc(stacks_free, 1)
                        for i, (stack, parts) in enumerate(((q_stack, Q_PART), (k_stack, K_PART))):
                            for p in range(PARTS):
                                sp.wait_ge(part_done[i][p][u], n)
                                for t in range(TERMS):
                                    if parts[t] == p:
                                        sp.dma_start(stack[u][t * RE:(t + 1) * RE], part[u][:, i, p]
                                                     ).then_inc(stacked[u], 16)
                for u in range(2):
                    sp.wait_ge(x1_ready[u], turn)
                    sp.dma_start(x1_all[:, bass.ds(unit[u], 1)], xh[u][:].unsqueeze(1)
                                 ).then_inc(x1_stored[u], 16)
            for u in range(2):
                sp.wait_ge(x1_stored[u], 16 * TURNS)

        @block.tensor
        def _(pe):
            pe.wait_ge(loaded, all_loaded)
            pe.wait_ge(turned_w, 1)

            def scores(u, n, j):
                s, h = j // RH, j % RH
                if j >= 2:
                    pe.wait_ge(s_masked[u], (n - 1) * HEADS + (j - 1))
                b = B(u, S_BANK[j % 2])
                t0 = s * L
                nc.tensor.matmul(b[:, 0:L], k_stack[u][0:RROWS, h, t0:t0 + P],
                                 q_stack[u][0:RROWS, h, t0:t0 + L], start=True, stop=True)
                nc.tensor.matmul(b[:, L:L + P], k_stack[u][0:RROWS, h, t0 + P:t0 + L],
                                 q_stack[u][0:RROWS, h, t0 + P:t0 + L], start=True, stop=True
                                 ).then_inc(s_mm[u], 1)

            def times_v(u, n, j):
                s, h = j // RH, j % RH
                pair, odd = h // 2, h % 2
                pe.wait_ge(s_masked[u], (n - 1) * HEADS + (j + 1))
                o = B(u, 1)[32 * pair:32 * pair + 32, s * L:(s + 1) * L]
                p = prob[u][j % PB]
                nc.tensor.matmul(o, v_pad[u][:, 2 * s, h], flat(p[:, 0:2]),
                                 start=(odd == 0), stop=False, skip_group_check=True)
                nc.tensor.matmul(o[:, P:L], v_pad[u][:, 2 * s + 1, h], p[:, 2],
                                 start=False, stop=(odd == 1), skip_group_check=True
                                 ).then_inc(pv_mm[u], 1)

            with pe.Fori(0, TURNS) as it:
                for l in range(LAYERS):
                    n = it * LAYERS + (l + 1)
                    for u in range(2):
                        pe.wait_ge(n1_done[u], n)
                        for c in range(NC):
                            t = nc.tensor.transpose(chunk(B(u, 0), c), xh[u][:, c], ident[:])
                        t.then_inc(n1_turn[u], 1)
                    for u in range(2):
                        pe.wait_ge(n1_hT[u], n)
                        for i, b, done in ((0, 1, q_mm), (1, 2, qt_mm), (2, 3, k_mm), (3, 0, kt_mm)):
                            nc.tensor.matmul(B(u, b)[:], flat(wqk[:, l, i]), hT[u][:], start=True, stop=True
                                             ).then_inc(done[u], 1)
                    for u in range(2):
                        pe.wait_ge(rotated[0][u], n)
                        for c in range(NC):
                            t = nc.tensor.matmul(chunk(B(u, 1), c), chunk(hT[u], c), flat(wv_s[:, l]),
                                                 start=True, stop=True)
                        t.then_inc(v_mm[u], 1)
                        for c in range(NC):
                            t = nc.tensor.matmul(chunk(B(u, 2), c), chunk(hT[u], c), wg_s[:, l],
                                                 start=True, stop=True)
                        t.then_inc(g_mm[u], 1)
                    for u in range(2):
                        pe.wait_ge(stacked[u], n * (16 * STACK_DMAS))
                        pe.wait_ge(rotated[1][u], n)
                        pe.wait_ge(v_ready[u], n)
                        for j in range(HEADS + 1):
                            if j < HEADS:
                                scores(u, n, j)
                            if j >= 1:
                                times_v(u, n, j - 1)
                    for u in range(2):
                        pe.wait_ge(y_done[u], n)
                        pe.wait_ge(gate_done[u], n)
                        for c in range(NC):
                            t = nc.tensor.transpose(chunk(B(u, 2), c), chunk(y[u], c), ident[:])
                        t.then_inc(y_turn[u], 1)
                    for u in range(2):
                        pe.wait_ge(z_done[u], n)
                        for c in range(NC):
                            t = nc.tensor.transpose(chunk(B(u, 3), c), dev[u][:, c], ident[:])
                        t.then_inc(z_turn[u], 1)
                    for u in range(2):
                        pe.wait_ge(zT_done[u], n)
                        for c in range(NC):
                            t = nc.tensor.matmul(chunk(B(u, 0), c), chunk(zT[u], c), wo_s[:, l],
                                                 start=True, stop=True)
                        t.then_inc(o_mm[u], 1)
                    for u in range(2):
                        pe.wait_ge(n2_done[u], n)
                        for c in range(NC):
                            t = nc.tensor.transpose(chunk(B(u, 1), c), xh[u][:, c], ident[:])
                        t.then_inc(n2_turn[u], 1)
                    for u in range(2):
                        pe.wait_ge(n2_hT[u], n)
                        for f in range(NF):
                            nc.tensor.matmul(B(u, F_BANK[f])[:], w1_s[:, l, f * P:(f + 1) * P], hT[u][:],
                                             start=True, stop=True).then_inc(f1_mm[f][u], 1)
                    for u in range(2):
                        for f in range(NF):
                            pe.wait_ge(gelu_done[f][u], n)
                        for c in range(NC):
                            for f in range(NF):
                                t = nc.tensor.matmul(chunk(B(u, 2), c), chunk(hidden[u][:, f], c), w2_s[:, l, f],
                                                     start=(f == 0), stop=(f == NF - 1))
                        t.then_inc(f2_mm[u], 1)

        @block.scalar
        def _(act):
            act.wait_ge(loaded, all_loaded)
            act.wait_ge(padded, 1)
            with act.Fori(0, TURNS) as it:
                for l in range(LAYERS):
                    n = it * LAYERS + (l + 1)
                    for u in range(2):
                        act.wait_ge(n1_turn[u], n)
                        nc.scalar.activation(hT[u][:], B(u, 0)[:], ACT.Identity, scale=ln_s[:, 0, l:l + 1],
                                             bias=ln_s[:, 1, l:l + 1]).then_inc(n1_hT[u], 1)
                    for u in range(2):
                        act.wait_ge(stacked[u], (n - 1) * (16 * STACK_DMAS))
                        for i in range(2):
                            act.wait_ge(full[i][u], n)
                            nc.scalar.activation(part[u][:, i, 0], qk[u][:, i], ACT.Copy
                                                 ).then_inc(part_done[i][0][u], 1)
                    for u in range(2):
                        act.wait_ge(v_mm[u], n)
                        v = B(u, 1)[:].rearrange("p (c r o e) -> p c r o e", c=NC, o=2, e=RE)
                        for odd in range(2):
                            a = nc.scalar.activation(v_pad[u][:, :, odd::2, odd * RE:(odd + 1) * RE], v[:, :, :, odd],
                                                     ACT.Copy)
                        a.then_inc(v_ready[u], 1)
                        act.wait_ge(g_mm[u], n)
                        nc.scalar.activation(gate_t[u][:], B(u, 2)[:], ACT.Tanh, scale=0.5).then_inc(tanh_done[u], 1)
                    for u in range(2):
                        for j in range(HEADS):
                            act.wait_ge(s_mm[u], (n - 1) * HEADS + (j + 1))
                            act.wait_ge(pv_mm[u], (n - 1) * HEADS + max(j - PB + 1, 0))
                            nc.scalar.activation(prob[u][j % PB][:, 1], B(u, S_BANK[j % 2])[:, P:L], ACT.Copy
                                                 ).then_inc(s_off[u], 1)
                    for u in range(2):
                        act.wait_ge(pv_mm[u], n * HEADS)
                        nc.scalar.activation(y[u][:], B(u, 1)[:], ACT.Copy).then_inc(y_done[u], 1)
                    for u in range(2):
                        act.wait_ge(g_dev[u], n)
                        nc.scalar.activation(gate_t[u][:], flat(dev[u]), ACT.Square).then_inc(g_sq[u], 1)
                        act.wait_ge(g_var[u], n)
                        nc.scalar.activation(g_sum[u][:], g_stat[u][:], ACT.Sqrt).then_inc(g_sd[u], 1)
                    for u in range(2):
                        act.wait_ge(z_turn[u], n)
                        nc.scalar.activation(zT[u][:], B(u, 3)[:], ACT.Copy).then_inc(zT_done[u], 1)
                    for u in range(2):
                        act.wait_ge(n2_turn[u], n)
                        nc.scalar.activation(hT[u][:], B(u, 1)[:], ACT.Identity, scale=ln_s[:, 2, l:l + 1],
                                             bias=ln_s[:, 3, l:l + 1]).then_inc(n2_hT[u], 1)
                    for u in range(2):
                        for f in range(NF):
                            act.wait_ge(f1_mm[f][u], n)
                            nc.scalar.activation(hidden[u][:, f], B(u, F_BANK[f])[:], ACT.Gelu,
                                                 bias=b1_s[:, l, f:f + 1]).then_inc(gelu_done[f][u], 1)

        @block.gpsimd
        def _(pool):
            nc.gpsimd.memset(minus_half[:], -0.5)
            nc.gpsimd.memset(eps[:], EPS)
            for u in range(2):
                t = nc.gpsimd.memset(v_pad[u][:], 0.0)
            t.then_inc(padded, 1)
            pool.wait_ge(padded, 1)
            pool.wait_ge(loaded, all_loaded)
            with pool.Fori(0, TURNS) as it:
                for l in range(LAYERS):
                    n = it * LAYERS + (l + 1)
                    for u in range(2):
                        inverse_root(nc, pool, mv[u], var[u], rstd[u], eps, minus_half, n_stat[u], n_var[u], n_root[u], norm_count(it, l))
                    for u in range(2):
                        pool.wait_ge(gate_done[u], n)
                        nc.gpsimd.tensor_tensor(gate_w[u][:], gate[u][:],
                                                gnw_s[:, l].unsqueeze(1).to_broadcast([P, NC, D]), ALU.mult)
                        nc.gpsimd.tensor_tensor(gate_b[u][:], gate[u][:],
                                                gnb_s[:, l].unsqueeze(1).to_broadcast([P, NC, D]), ALU.mult
                                                ).then_inc(gates_done[u], 1)
                    for u in range(2):
                        inverse_root(nc, pool, mv[u], var[u], rstd[u], eps, minus_half, n_stat[u], n_var[u], n_root[u], norm_count(it, l, 1))
                        nc.gpsimd.tensor_tensor(resb[u][:], res[u][:],
                                                b2_s[:, l].unsqueeze(1).to_broadcast([P, NC, D]), ALU.add
                                                ).then_inc(resb_done[u], 1)
                for u in range(2):
                    inverse_root(nc, pool, mv[u], var[u], rstd[u], eps, minus_half, n_stat[u], n_var[u], n_root[u], norm_count(it, LAYERS))

        @block.vector
        def _(dve):
            dve.wait_ge(loaded, all_loaded)
            for l in range(LAYERS):
                for i in range(2):
                    src = wqk_raw[:, l, i].rearrange("p h e -> p e h")
                    nc.vector.tensor_copy(wqk[:, l, 2 * i], src)
                    nc.vector.tensor_scalar(wqk[:, l, 2 * i + 1, 0::2], src[:, 1::2], -1.0, None, ALU.mult)
                    t = nc.vector.tensor_copy(wqk[:, l, 2 * i + 1, 1::2], src[:, 0::2])
            t.then_inc(turned_w, 1)

            def by_seq(t):
                return t.rearrange("p (s t) -> p s t", s=SPU)

            def by_head(t):
                return t.rearrange("p (g e) -> p g e", e=RE)

            def per_head(t):
                return t[:].unsqueeze(2).to_broadcast([P, NC * RH, RE])

            with dve.Fori(0, TURNS) as it:
                for l in range(LAYERS):
                    n = it * LAYERS + (l + 1)
                    src = xin if l == 0 else res
                    for u in range(2):
                        if l == 0:
                            dve.wait_ge(x_in[u], (it + 1) * 16)
                            dve.wait_ge(x1_stored[u], it * 16)
                        else:
                            dve.wait_ge(f_res[u], n - 1)
                        layer_norm_stats(nc, dve, src[u], bn[u], mv[u], n_half[u], n_seen[u], n_stat[u], norm_count(it, l))
                    for u in range(2):
                        normalise(nc, dve, src[u], xh[u], mv[u], rstd[u], n_root[u], norm_count(it, l), n1_done[u])
                    for u in range(2):
                        for i in range(2):
                            cos = xpos[:, 2 * i].unsqueeze(1).to_broadcast([P, SPU, L])
                            sin = xpos[:, 2 * i + 1].unsqueeze(1).to_broadcast([P, SPU, L])
                            if i == 1:
                                dve.wait_ge(full[0][u], n)
                            dve.wait_ge(mm_of[i][0][u], n)
                            nc.vector.tensor_tensor(by_seq(rot_a[u][:]), by_seq(B(u, (1, 3)[i])[:]), cos, ALU.mult)
                            dve.wait_ge(mm_of[i][1][u], n)
                            nc.vector.tensor_tensor(by_seq(rot_b[u][:]), by_seq(B(u, (2, 0)[i])[:]), sin, ALU.mult
                                                    ).then_inc(rotated[i][u], 1)
                            dve.wait_ge(rotated[i][u], n)
                            nc.vector.tensor_tensor(qk[u][:, i], rot_a[u][:], rot_b[u][:], ALU.add
                                                    ).then_inc(full[i][u], 1)
                        for i in range(2):
                            dve.wait_ge(part_done[i][0][u], n)
                            nc.vector.tensor_tensor(qk[u][:, i], qk[u][:, i], part[u][:, i, 0], ALU.subtract
                                                    ).then_inc(part_left[i][u], 1)
                            dve.wait_ge(part_left[i][u], n)
                            nc.vector.tensor_copy(part[u][:, i, 1], qk[u][:, i]).then_inc(part_done[i][1][u], 1)
                            dve.wait_ge(part_done[i][1][u], n)
                            nc.vector.tensor_tensor(part[u][:, i, 2], qk[u][:, i], part[u][:, i, 1], ALU.subtract
                                                    ).then_inc(part_done[i][2][u], 1)
                    for u in range(2):
                        dve.wait_ge(tanh_done[u], n)
                        nc.vector.scalar_tensor_tensor(flat(gate[u]), gate_t[u][:], 1.0, B(u, 2)[:], ALU.add, ALU.mult
                                                       ).then_inc(gate_done[u], 1)
                    for u in range(2):
                        for j in range(HEADS):
                            dve.wait_ge(s_off[u], (n - 1) * HEADS + (j + 1))
                            s = B(u, S_BANK[j % 2])[:, 0:3 * P].rearrange("p (a b) -> p a b", b=P)
                            nc.vector.tensor_tensor(prob[u][j % PB][:, 0::2], s[:, 0::2],
                                                    mask[:].unsqueeze(1).to_broadcast([P, 2, P]), ALU.mult
                                                    ).then_inc(s_masked[u], 1)
                    for u in range(2):
                        dve.wait_ge(y_turn[u], n)
                        nc.vector.tensor_reduce(g_sum[u][:], by_head(B(u, 2)[:]), AX.X, ALU.add
                                                ).then_inc(g_sum_done[u], 1)
                        dve.wait_ge(g_sum_done[u], n)
                        nc.vector.tensor_scalar(g_stat[u][:], g_sum[u][:], 1.0 / RE, None, ALU.mult
                                                ).then_inc(g_mean[u], 1)
                        dve.wait_ge(g_mean[u], n)
                        nc.vector.tensor_tensor(by_head(flat(dev[u])), by_head(B(u, 2)[:]), per_head(g_stat[u]),
                                                ALU.subtract).then_inc(g_dev[u], 1)
                    for u in range(2):
                        dve.wait_ge(g_sq[u], n)
                        nc.vector.tensor_reduce(g_sum[u][:], by_head(gate_t[u][:]), AX.X, ALU.add
                                                ).then_inc(g_sqsum[u], 1)
                        dve.wait_ge(g_sqsum[u], n)
                        nc.vector.tensor_scalar(g_stat[u][:], g_sum[u][:], 1.0 / RE, EPS, ALU.mult, ALU.add
                                                ).then_inc(g_var[u], 1)
                    for u in range(2):
                        dve.wait_ge(g_sd[u], n)
                        nc.vector.reciprocal(g_stat[u][:], g_sum[u][:]).then_inc(g_root[u], 1)
                        dve.wait_ge(g_root[u], n)
                        nc.vector.tensor_tensor(by_head(y[u][:]), by_head(flat(dev[u])), per_head(g_stat[u]), ALU.mult
                                                ).then_inc(g_norm[u], 1)
                        dve.wait_ge(g_norm[u], n)
                        dve.wait_ge(gates_done[u], n)
                        nc.vector.scalar_tensor_tensor(y[u][:], y[u][:], 0.5, flat(gate_w[u]), ALU.mult, ALU.mult
                                                       ).then_inc(g_scaled[u], 1)
                        dve.wait_ge(g_scaled[u], n)
                        nc.vector.scalar_tensor_tensor(flat(dev[u]), flat(gate_b[u]), 0.5, y[u][:], ALU.mult, ALU.add
                                                       ).then_inc(z_done[u], 1)
                    for u in range(2):
                        dve.wait_ge(o_mm[u], n)
                        nc.vector.tensor_tensor(flat(res[u]), B(u, 0)[:], flat(src[u]), ALU.add
                                                ).then_inc(o_res[u], 1)
                        dve.wait_ge(o_res[u], n)
                        layer_norm_stats(nc, dve, res[u], bn[u], mv[u], n_half[u], n_seen[u], n_stat[u], norm_count(it, l, 1))
                    for u in range(2):
                        normalise(nc, dve, res[u], xh[u], mv[u], rstd[u], n_root[u], norm_count(it, l, 1), n2_done[u])
                    for u in range(2):
                        dve.wait_ge(f2_mm[u], n)
                        dve.wait_ge(resb_done[u], n)
                        nc.vector.tensor_tensor(flat(res[u]), B(u, 2)[:], flat(resb[u]), ALU.add
                                                ).then_inc(f_res[u], 1)
                for u in range(2):
                    dve.wait_ge(f_res[u], (it + 1) * LAYERS)
                    nc.vector.tensor_tensor(resb[u][:], res[u][:], xin[u][:], ALU.add).then_inc(x_summed[u], 1)
                    dve.wait_ge(x_summed[u], it + 1)
                    layer_norm_stats(nc, dve, resb[u], bn[u], mv[u], n_half[u], n_seen[u], n_stat[u], norm_count(it, LAYERS))
                for u in range(2):
                    normalise(nc, dve, resb[u], xh[u], mv[u], rstd[u], n_root[u], norm_count(it, LAYERS), x1_ready[u])
    return used


def attention_block(nc, bank, x1_all, out, ln_g, ln_b, wq, wk, wv, wo, w1, b1, w2, b2, c_ident):
    out_units = out.rearrange("(n s) (h p) d -> p n (s h) d", s=SPU, p=P)
    SLOTS = 2 * SPU * TILES
    FIRST, LEAD = 6, 10
    FILLS = 4
    PAIR_TILES = SPU * TILES
    QROWS = AE * TERMS * QUADS
    LN_AT, TURN_AT, Q_AT, K_AT, V_AT, PARTS_AT = (3, 18), (5, 20), (6, 21), (7, 22), (11, 27), (10, 26)
    O_AT, OT_AT, F1_AT, F2_AT = (13, 29), (14, 30), (15, 31), (16, 31)
    MAX_AT = {0: 1, 8: 2, 16: 3, 24: 4}
    ATT_AT = {3: 0, 11: 1, 19: 2, 27: 3}

    with ExitStack() as ctx:
        def sb(name, shape, dt=F32):
            return ctx.enter_context(nc.sbuf_tensor(name, shape, dt))

        def two(name, shape, dt=F32):
            return [sb(f"{name}{u}", shape, dt) for u in range(2)]

        sem = nc.alloc_semaphore

        ident = sb("a_ident", [P, P])
        ident_bf = sb("a_ident_bf", [P, P], BF16)
        minus_half, eps = sb("a_minus_half", [P, NC]), sb("a_eps", [P, NC])
        minus_one, zero = sb("minus_one", [P, 2, QUADS, TILES]), sb("zero", [P, 2, QUADS, TILES])
        g_s = sb("g_s", [P, 2])
        wqk_raw = sb("a_wqk_raw", [P, 2, D])
        wqk_p = sb("wqk_p", [P, 2, QUADS, AE, TILES])
        wv_s = sb("a_wv", [P, D])
        wo_p = sb("wo_p", [P, D])
        w1_s, w2_s = two("a_w1", [P, FFN]), two("a_w2", [P, NF, D])
        b1_s, b2_s = two("a_b1", [P, NF]), two("a_b2", [P, D])

        x_ln = sb("x_ln", [P, NC, D])
        bn, mv, var, rstd = sb("a_bn", [P, NC, 6]), sb("a_mv", [P, NC, 2]), sb("a_var", [P, NC]), sb("a_rstd", [P, NC])
        xh = sb("a_xh", [P, NC, D])
        hT = sb("a_hT", [P, UNIT])
        left = sb("left", [P, UNIT])
        part = sb("a_part", [P, 2, PARTS, UNIT], BF16)
        q_bd = two("q_bd", [P, TILES, QUADS, UNIT], BF16)
        k_dense = two("k_dense", [P, TILES, UNIT], BF16)
        v_ones = two("v_ones", [P, NC, AH, VW])
        mx = two("mx", [P, 2, TILES, QUADS])
        m_neg, m_left = sb("m_neg", [P, 2, QUADS, TILES]), sb("m_left", [P, 2, QUADS, TILES])
        m_part = sb("m_part", [P, 2, P], BF16)
        mT = sb("mT", [P, L], BF16)
        prob = two("a_prob", [P, 2, QUADS, L])
        pv_s = sb("pv_s", [P, TILES, L])
        att_n, att_d = sb("att_n", [P, UNIT]), sb("att_d", [P, UNIT])
        att_r, att = sb("att_r", [P, UNIT]), sb("att", [P, UNIT])
        x_res, x_b2 = sb("x_res", [P, NC, D]), sb("x_b2", [P, NC, D])
        o_s, oT = sb("o_s", [P, NC, D]), sb("oT", [P, UNIT])
        hidden = sb("a_hidden", [P, NF, UNIT])
        y_s, y_out = sb("y_s", [P, NC, D]), sb("y_out", [P, NC, D])
        bn2, mv2, var2, rstd2 = (sb("a_bn2", [P, NC, 6]), sb("a_mv2", [P, NC, 2]), sb("a_var2", [P, NC]),
                                 sb("a_rstd2", [P, NC]))

        loaded, ready_dve, ready_pool = sem("a_loaded"), sem("a_ready_dve"), sem("a_ready_pool")
        x_ln_in, n_half, n_seen, n_stat, n_var, n_root, xh_done = map(sem, (
            "x_ln_in", "an_half", "an_seen", "an_stat", "an_var", "an_root", "xh_done"))
        x_turn, hT_done = sem("x_turn"), sem("hT_done")
        qk_mm = [sem("aq_mm"), sem("ak_mm")]
        part_done = [[sem(f"a{q}_part{i}") for i in range(PARTS)] for q in "qk"]
        part_left = [sem("aq_left"), sem("ak_left")]
        parts_free, stacked = sem("parts_free"), sem("a_stacked")
        v_mm, v_ready = sem("av_mm"), sem("av_ready")
        a_mm, a_max, b_mm, b_exp, pv_mm, pv_out, pv_moved = map(sem, (
            "a_mm", "a_max", "b_mm", "b_exp", "apv_mm", "pv_out", "pv_moved"))
        m_neg_done, m_part0, m_left_done, m_part1, m_part2, m_turn, mT_done, m_in = map(sem, (
            "m_neg_done", "m_part0", "m_left_done", "m_part1", "m_part2", "m_turn", "mT_done", "m_in"))
        sums_inv, att_done, o_mm, x_res_in, o_done, o_turn, oT_done = map(sem, (
            "sums_inv", "att_done", "ao_mm", "x_res_in", "o_done", "o_turn", "oT_done"))
        w_in, f1_mm, gelu, f2_mm, x_b2_done, y_sum = map(sem, (
            "w_in", "af1_mm", "a_gelu", "af2_mm", "x_b2_done", "y_sum"))
        n2_half, n2_seen, n2_stat, n2_var, n2_root, y_ready, stored, sp_seen = map(sem, (
            "n2_half", "n2_seen", "n2_stat", "n2_var", "n2_root", "y_ready", "stored", "sp_seen"))
        W_DMAS = 4

        def wait(eng, s, n):
            if not isinstance(n, int) or n > 0:
                eng.wait_ge(s, n)

        def chunk(t, c):
            return t[:, c * P:(c + 1) * P]

        def where(T):
            return (T // PAIR_TILES) % 2, (T // TILES) % SPU, T % TILES

        A_BANK = bank[0:2]
        B_BANK = bank[2:5]
        PV_BANK, PREP, TAIL = bank[5], bank[6], bank[7]

        loads = [(ident[:], c_ident), (wqk_raw[:, 0], wq), (wqk_raw[:, 1], wk), (wv_s[:], wv),
                 (g_s[:, 0:1], ln_g.rearrange("(p a) -> p a", a=1)), (g_s[:, 1:2], ln_b.rearrange("(p a) -> p a", a=1))]
        wo_rows = wo.rearrange("(t j d) n -> j d t n", j=QUADS, d=AE)
        for j in range(QUADS):
            for d in range(AE):
                r = (j * AE + d) * TILES
                loads.append((wo_p[r:r + TILES], wo_rows[j, d]))
        all_loaded = 16 * len(loads)

        block = ctx.enter_context(nc.Block())

        @block.sync
        def _(sp):
            for dst, src in loads:
                with nc.allow_non_contiguous_dma("weights, once"):
                    sp.dma_start(dst, src).then_inc(loaded, 16)

            def load_x_ln(p):
                p, n = sp.snap(p), sp.snap(p * 1)
                wait(sp, xh_done, n)
                sp.dma_start(x_ln[:].unsqueeze(1), x1_all[:, bass.ds(p, 1)]).then_inc(x_ln_in, 16)

            def load_x_res(p):
                p, n = sp.snap(p), sp.snap(p * 1)
                wait(sp, o_done, n)
                sp.sem_inc(sp_seen, 1)
                wait(sp, x_b2_done, n)
                sp.dma_start(x_res[:].unsqueeze(1), x1_all[:, bass.ds(p, 1)]).then_inc(x_res_in, 16)

            def load_expert(p, e, u):
                e = sp.snap(e)
                if u == 1 or not isinstance(p, int):
                    wait(sp, f2_mm, p - 1)
                    sp.sem_inc(sp_seen, 1)
                    wait(sp, x_b2_done, p - 1)
                    sp.sem_inc(sp_seen, 1)
                with nc.allow_non_contiguous_dma("bias by feature"):
                    sp.dma_start(w1_s[u][:].unsqueeze(1), w1.rearrange("e p n -> p e n")[:, bass.ds(e, 1)]
                                 ).then_inc(w_in, 16)
                    sp.dma_start(w2_s[u][:].unsqueeze(1), w2.rearrange("e (f p) n -> p e f n", p=P)[:, bass.ds(e, 1)]
                                 ).then_inc(w_in, 16)
                    sp.dma_start(b1_s[u][:].unsqueeze(1), b1.rearrange("e (f p) -> p e f", p=P)[:, bass.ds(e, 1)]
                                 ).then_inc(w_in, 16)
                    sp.dma_start(b2_s[u][:], b2[bass.ds(e, 1)].to_broadcast([P, D])).then_inc(w_in, 16)

            def spread_parts(p, u):
                n = p + 1
                wait(sp, b_mm, (p - 1) * (PAIR_TILES * FILLS))
                sp.sem_inc(parts_free, 1)
                for i, parts in ((1, K_PART), (0, Q_PART)):
                    for c in sorted(range(TERMS), key=lambda c: parts[c]):
                        wait(sp, part_done[i][parts[c]], n)
                        if i == 1:
                            sp.dma_start(k_dense[u][c:QROWS:TERMS], part[:, 1, parts[c]]).then_inc(stacked, 16)
                        else:
                            for j in range(QUADS):
                                r = QROWS // QUADS
                                sp.dma_start(q_bd[u][r * j + c:r * (j + 1):TERMS, :, j],
                                             part[32 * j:32 * (j + 1), 0, parts[c]]).then_inc(stacked, 16)

            def spread_max(h, u, s):
                wait(sp, mT_done, h + 1)
                sp.sem_inc(sp_seen, 1)
                for j in range(QUADS):
                    sp.dma_start(q_bd[u][QROWS + PARTS * j:QROWS + PARTS * (j + 1), :, j, s * L:(s + 1) * L],
                                 mT[j * PARTS * TILES:(j + 1) * PARTS * TILES]).then_inc(m_in, 16)

            def collect(h, s):
                wait(sp, att_done, h if s == 0 else h - 1)
                sp.sem_inc(sp_seen, 1)
                wait(sp, pv_out, (h + 1) * (TILES // 2))
                for j in range(QUADS):
                    for k, dst in enumerate((att_n, att_d)):
                        sp.dma_start(dst[32 * j:32 * (j + 1), s * L:(s + 1) * L],
                                     pv_s[32 * j + AE * k:32 * j + AE * (k + 1)]).then_inc(pv_moved, 16)

            def store(p):
                p, n = sp.snap(p), sp.snap(p + 1)
                wait(sp, y_ready, n)
                sp.dma_start(out_units[:, bass.ds(p, 1)], y_out[:].unsqueeze(1)).then_inc(stored, 16)

            def slots(it, last):
                for k in range(SLOTS):
                    if k in MAX_AT and not (last and MAX_AT[k] > 3):
                        g = MAX_AT[k]
                        spread_max(it * 4 + g, (g // 2) % 2, g % 2)
                    if k in ATT_AT:
                        collect(it * 4 + ATT_AT[k], ATT_AT[k] % 2)
                    if k == 1 and not last:
                        load_x_ln(it * 2 + 2)
                    if k == 16 and not last:
                        load_x_ln(it * 2 + 3)
                    if k == 4:
                        load_x_res(it * 2)
                    if k == 20:
                        load_x_res(it * 2 + 1)
                    if k == 4:
                        load_expert(it * 2 + 1, (it * 2 + 1) % EXPERTS, 1)
                    if k == 24 and not last:
                        load_expert(it * 2 + 2, (it * 2 + 2) % EXPERTS, 0)
                    for u in range(2):
                        if k == PARTS_AT[u] and not last:
                            spread_parts(it * 2 + 2 + u, u)
                    if k == F2_AT[0] + 3:
                        store(it * 2)
                    if k == SLOTS - 1:
                        store(it * 2 + 1)

            load_x_ln(0)
            load_expert(0, 0, 0)
            spread_parts(0, 0)
            load_x_ln(1)
            spread_parts(1, 1)
            spread_max(0, 0, 0)
            with sp.Fori(0, TURNS - 1) as it:
                slots(it, False)
            slots(TURNS - 1, True)
            sp.wait_ge(stored, 16 * UNITS)

        @block.tensor
        def _(pe):
            pe.wait_ge(loaded, all_loaded)
            pe.wait_ge(ready_dve, 1)
            pe.wait_ge(ready_pool, 1)

            def prep_turn(p):
                wait(pe, xh_done, p + 1)
                wait(pe, v_ready, p)
                wait(pe, mT_done, 1 if isinstance(p, int) and p == 2 else 0)
                for c in range(NC):
                    t = nc.tensor.transpose(chunk(PREP, c), xh[:, c], ident[:])
                t.then_inc(x_turn, 1)

            def prep_qk(p, i):
                wait(pe, hT_done, p + 1)
                if i == 1:
                    wait(pe, part_left[0], p + 1)
                nc.tensor.matmul(PREP[:], wqk_p[:, i].rearrange("p j d t -> p (j d t)"), hT[:], start=True, stop=True
                                 ).then_inc(qk_mm[i], 1)

            def prep_v(p):
                wait(pe, part_left[1], p + 1)
                for c in range(NC):
                    t = nc.tensor.matmul(chunk(PREP, c), chunk(hT, c), wv_s[:], start=True, stop=True)
                t.then_inc(v_mm, 1)

            def turn_max(h):
                wait(pe, m_part2, h + 1)
                for q in range(2):
                    t = nc.tensor.matmul(chunk(PREP, q), m_part[:, q], ident_bf[:], start=True, stop=True)
                t.then_inc(m_turn, 1)

            def a_fill(it, a, f):
                u, s, t = where(a)
                n = (it * SLOTS + a) * FILLS + f
                if f == 0 and t == 0 and s == 0:
                    wait(pe, stacked, (it * 2 + (a // PAIR_TILES + 1)) * (16 * TERMS * (1 + QUADS)))
                wait(pe, a_max, n - 1)
                for i in range(2):
                    j = 2 * (f % 2) + i
                    q0 = s * L + (f // 2) * P
                    m = nc.tensor.matmul(A_BANK[f % 2][:, i * L:(i + 1) * L], q_bd[u][0:QROWS, t, j, q0:q0 + P],
                                         k_dense[u][0:QROWS, t, s * L:(s + 1) * L], start=True, stop=True)
                m.then_inc(a_mm, 1)

            def b_fill(it, T, f):
                u, s, t = where(T)
                n = T * FILLS + f
                if f == 0 and t == 0:
                    wait(pe, m_in, (it * 4 + (T // TILES + 1)) * (16 * QUADS))
                prev = n - 2 if n >= FIRST * FILLS + 3 else min(n, FIRST * FILLS)
                if n < 24:
                    prev = n - 2
                wait(pe, b_exp, it * (SLOTS * FILLS) + prev)
                j, k0 = 2 * (f % 2), s * L + (f // 2) * P
                nc.tensor.matmul(B_BANK[n % 3][:], k_dense[u][:, t, k0:k0 + P],
                                 q_bd[u][:, t, j:j + 2, s * L:(s + 1) * L], start=True, stop=True).then_inc(b_mm, 1)

            def times_v(it, T):
                u, s, t = where(T)
                n = it * SLOTS + T
                wait(pe, b_exp, (n + 1) * FILLS)
                if T % 2 == 0:
                    wait(pe, pv_out, it * (SLOTS // 2) + T // 2)
                if t == 0 and s == 0:
                    wait(pe, v_ready, it * 2 + (T // PAIR_TILES + 1))
                for k in range(2):
                    for j in range(QUADS):
                        m = nc.tensor.matmul(PV_BANK[32 * j:32 * j + VW, (T % 2) * L:(T % 2 + 1) * L],
                                             v_ones[u][:, 2 * s + k, QUADS * t + j], prob[T % 2][:, k, j],
                                             start=(k == 0), stop=(k == 1), skip_group_check=True)
                m.then_inc(pv_mm, 1)

            def project(p):
                wait(pe, att_done, p * 2 + 2)
                wait(pe, y_sum, p)
                for c in range(NC):
                    t = nc.tensor.matmul(chunk(TAIL, c), chunk(att, c), wo_p[:], start=True, stop=True)
                t.then_inc(o_mm, 1)

            def turn_o(p):
                wait(pe, o_done, p + 1)
                for c in range(NC):
                    t = nc.tensor.transpose(chunk(TAIL, c), o_s[:, c], ident[:])
                t.then_inc(o_turn, 1)

            def expert_in(p, u, f, bank_read, n_read):
                if f == 0:
                    wait(pe, w_in, (p + 1) * (16 * W_DMAS))
                    wait(pe, bank_read, n_read)
                wait(pe, oT_done, p + 1)
                if f >= 2:
                    wait(pe, gelu, p * NF + (f - 1))
                nc.tensor.matmul((PREP, TAIL)[f % 2][:], w1_s[u][:, f * P:(f + 1) * P], oT[:], start=True, stop=True
                                 ).then_inc(f1_mm, 1)

            def expert_out(p, u):
                wait(pe, gelu, (p + 1) * NF)
                for c in range(NC):
                    for f in range(NF):
                        t = nc.tensor.matmul(chunk(TAIL, c), chunk(hidden[:, f], c), w2_s[u][:, f],
                                             start=(f == 0), stop=(f == NF - 1))
                t.then_inc(f2_mm, 1)

            def slots(it, last):
                for k in range(SLOTS):
                    T, a = FIRST + k, FIRST + LEAD + k
                    for f in range(FILLS):
                        for u in range(2):
                            p = it * 2 + 2 + u
                            if f == 0 and not last:
                                if k == TURN_AT[u]:
                                    wait(pe, mT_done, it * 4 + (2, 4)[u])
                                    if u == 1:
                                        wait(pe, gelu, it * (2 * NF) + 3)
                                    prep_turn(p)
                                if k == Q_AT[u]:
                                    prep_qk(p, 0)
                                if k == K_AT[u]:
                                    prep_qk(p, 1)
                                if k == V_AT[u]:
                                    wait(pe, mT_done, it * 4 + (3, 5)[u])
                                    prep_v(p)
                            p = it * 2 + u
                            if f == 0 and k == O_AT[u]:
                                project(p)
                            if f == 0 and k == OT_AT[u]:
                                turn_o(p)
                            if k == F1_AT[u]:
                                if last:
                                    expert_in(p, u, f, mT_done, it * 4 + (3, 4)[u])
                                else:
                                    expert_in(p, u, f, v_ready, it * 2 + 3 + u)
                        if f == 0 and k in MAX_AT and not (last and MAX_AT[k] > 3):
                            if k == 0:
                                wait(pe, gelu, it * (2 * NF))
                                wait(pe, mT_done, it * 4 + 1)
                            if k == 8 and not last:
                                wait(pe, part_left[1], it * 2 + 3)
                            if k == 16:
                                wait(pe, gelu, it * (2 * NF) + 3)
                            if k == 24:
                                wait(pe, part_left[1], it * 2 + 4)
                            turn_max(it * 4 + MAX_AT[k])
                        if not (last and T >= SLOTS):
                            b_fill(it, T, f)
                        if not (last and a >= SLOTS):
                            a_fill(it, a, f)
                        if f == 1 and not (last and T > SLOTS):
                            times_v(it, T - 1)
                    for u in range(2):
                        if k == F2_AT[u]:
                            expert_out(it * 2 + u, u)

            for p in range(2):
                prep_turn(p)
                prep_qk(p, 0)
                prep_qk(p, 1)
                prep_v(p)
            for T in range(-LEAD, FIRST):
                if T + LEAD == TILES:
                    wait(pe, v_ready, 2)
                    turn_max(0)
                for f in range(FILLS):
                    if T >= 0:
                        b_fill(0, T, f)
                    a_fill(0, T + LEAD, f)
                    if f == 1 and T >= 1:
                        times_v(0, T - 1)
            with pe.Fori(0, TURNS - 1) as it:
                slots(it, False)
            slots(TURNS - 1, True)

        @block.scalar
        def _(act):
            act.wait_ge(loaded, all_loaded)
            act.wait_ge(ready_dve, 1)
            act.wait_ge(ready_pool, 1)

            def scale_hT(p):
                wait(act, x_turn, p + 1)
                nc.scalar.activation(hT[:], PREP[:], ACT.Identity, scale=g_s[:, 0:1], bias=g_s[:, 1:2]
                                     ).then_inc(hT_done, 1)

            def first_part(p, i):
                if i == 0:
                    wait(act, stacked, p * (16 * TERMS * (1 + QUADS)))
                wait(act, qk_mm[i], p + 1)
                nc.scalar.activation(part[:, i, 0], PREP[:], ACT.Copy).then_inc(part_done[i][0], 1)

            def second_part(p, i):
                wait(act, part_left[i], p + 1)
                nc.scalar.activation(part[:, i, 1], left[:], ACT.Copy).then_inc(part_done[i][1], 1)

            def keep_v(p, u):
                wait(act, v_mm, p + 1)
                wait(act, pv_mm, (p - 1) * PAIR_TILES)
                nc.scalar.activation(v_ones[u][:, :, :, 0:AE], PREP[:].rearrange("p (c h d) -> p c h d", c=NC, d=AE),
                                     ACT.Copy).then_inc(v_ready, 1)

            def keep_max(h):
                wait(act, m_in, h * (16 * QUADS))
                wait(act, m_turn, h + 1)
                nc.scalar.activation(mT[:], PREP[:, 0:L], ACT.Copy).then_inc(mT_done, 1)

            def exp(it, T, f):
                n = T * FILLS + f
                wait(act, b_mm, it * (SLOTS * FILLS) + (n + 1))
                if f == 0:
                    wait(act, pv_mm, it * SLOTS + (T - 1))
                j = 2 * (f % 2)
                nc.scalar.activation(prob[T % 2][:, f // 2, j:j + 2].rearrange("p j q -> p (j q)"), B_BANK[n % 3][:],
                                     ACT.Exp, scale=AE ** -0.5).then_inc(b_exp, 1)

            def keep_pv(it, T):
                t = T % TILES
                if t == 1:
                    wait(act, pv_moved, (it * 4 + T // TILES) * (16 * 2 * QUADS))
                wait(act, pv_mm, it * SLOTS + (T + 1))
                nc.scalar.activation(pv_s[:, t - 1:t + 1].rearrange("p t q -> p (t q)"), PV_BANK[:], ACT.Copy
                                     ).then_inc(pv_out, 1)

            def keep_oT(p):
                wait(act, o_turn, p + 1)
                wait(act, f1_mm, p * NF)
                nc.scalar.activation(oT[:], TAIL[:], ACT.Copy).then_inc(oT_done, 1)

            def gelus(p, u):
                wait(act, f2_mm, p)
                for f in range(NF):
                    wait(act, f1_mm, p * NF + (f + 1))
                    nc.scalar.activation(hidden[:, f], (PREP, TAIL)[f % 2][:], ACT.Gelu, bias=b1_s[u][:, f:f + 1]
                                         ).then_inc(gelu, 1)

            def slots(it, last):
                for k in range(SLOTS):
                    T = FIRST + k
                    for u in range(2):
                        p = it * 2 + 2 + u
                        if not last:
                            if k == TURN_AT[u]:
                                scale_hT(p)
                            for i, at in enumerate((Q_AT, K_AT)):
                                if k == at[u]:
                                    first_part(p, i)
                            if k == V_AT[u]:
                                keep_v(p, u)
                        if k == OT_AT[u]:
                            keep_oT(it * 2 + u)
                        if k == F1_AT[u]:
                            gelus(it * 2 + u, u)
                    if k in MAX_AT and not (last and MAX_AT[k] > 3):
                        keep_max(it * 4 + MAX_AT[k])
                    for f in range(FILLS):
                        if not (last and T >= SLOTS):
                            exp(it, T, f)
                        if f == 1:
                            for u in range(2):
                                for i, at in enumerate((Q_AT, K_AT)):
                                    if k == at[u] and not last:
                                        second_part(it * 2 + 2 + u, i)
                        if f == 2 and T % 2 == 0 and not (last and T > SLOTS):
                            keep_pv(it, T - 1)

            for p in range(2):
                scale_hT(p)
                for i in range(2):
                    first_part(p, i)
                    second_part(p, i)
                keep_v(p, p)
            for T in range(-LEAD, FIRST):
                if T + LEAD == TILES:
                    keep_max(0)
                for f in range(FILLS):
                    if T >= 0:
                        exp(0, T, f)
                    if f == 2 and T >= 1 and T % 2 == 0:
                        keep_pv(0, T - 1)
            with act.Fori(0, TURNS - 1) as it:
                slots(it, False)
            slots(TURNS - 1, True)

        @block.gpsimd
        def _(pool):
            nc.gpsimd.memset(minus_half[:], -0.5)
            nc.gpsimd.memset(eps[:], EPS)
            nc.gpsimd.memset(minus_one[:], -1.0)
            nc.gpsimd.memset(zero[:], 0.0)
            nc.gpsimd.memset(m_part[:], 0.0)
            for u in range(2):
                t = nc.gpsimd.memset(v_ones[u][:], 1.0)
            t.then_inc(ready_pool, 1)
            pool.wait_ge(ready_pool, 1)

            def norm_root(p):
                inverse_root(nc, pool, mv, var, rstd, eps, minus_half, n_stat, n_var, n_root, p + 1)

            def third_part(p, i):
                wait(pool, part_done[i][1], p + 1)
                nc.gpsimd.tensor_tensor(part[:, i, 2], left[:], part[:, i, 1], ALU.subtract
                                        ).then_inc(part_done[i][2], 1)

            def split_max(h, par):
                def parts(c):
                    return m_part[:, :, 0:PARTS * QUADS * TILES].rearrange(
                        "p q (j c t) -> p q j c t", j=QUADS, c=PARTS)[:, :, :, c]
                src = mx[par][:].rearrange("p q t j -> p q j t")
                wait(pool, a_max, (h + 1) * (TILES * FILLS))
                nc.gpsimd.tensor_tensor(m_neg[:], src, minus_one[:], ALU.mult).then_inc(m_neg_done, 1)
                wait(pool, m_turn, h)
                nc.gpsimd.tensor_tensor(parts(0), src, minus_one[:], ALU.mult).then_inc(m_part0, 1)
                wait(pool, m_neg_done, h + 1)
                wait(pool, m_part0, h + 1)
                nc.gpsimd.tensor_tensor(m_left[:], m_neg[:], parts(0), ALU.subtract).then_inc(m_left_done, 1)
                wait(pool, m_left_done, h + 1)
                nc.gpsimd.tensor_tensor(parts(1), m_left[:], zero[:], ALU.add).then_inc(m_part1, 1)
                wait(pool, m_part1, h + 1)
                nc.gpsimd.tensor_tensor(parts(2), m_left[:], parts(1), ALU.subtract).then_inc(m_part2, 1)

            def add_b2(p, u):
                wait(pool, x_res_in, (p + 1) * 16)
                wait(pool, w_in, (p + 1) * (16 * W_DMAS))
                wait(pool, y_sum, p)
                nc.gpsimd.tensor_tensor(x_b2[:], x_res[:], b2_s[u][:].unsqueeze(1).to_broadcast([P, NC, D]), ALU.add
                                        ).then_inc(x_b2_done, 1)

            def out_root(p):
                inverse_root(nc, pool, mv2, var2, rstd2, eps, minus_half, n2_stat, n2_var, n2_root, p + 1)

            def slots(it, last):
                for k in range(SLOTS):
                    if k in MAX_AT and not (last and MAX_AT[k] > 3):
                        split_max(it * 4 + MAX_AT[k], MAX_AT[k] % 2)
                    for u in range(2):
                        if not last:
                            p = it * 2 + 2 + u
                            if k == LN_AT[u]:
                                norm_root(p)
                            for i, at in enumerate((Q_AT, K_AT)):
                                if k == at[u]:
                                    third_part(p, i)
                        if k == O_AT[u] - 1:
                            add_b2(it * 2 + u, u)
                        if k == F2_AT[u]:
                            out_root(it * 2 + u)

            for p in range(2):
                norm_root(p)
                for i in range(2):
                    third_part(p, i)
            split_max(0, 0)
            with pool.Fori(0, TURNS - 1) as it:
                slots(it, False)
            slots(TURNS - 1, True)

        @block.vector
        def _(dve):
            dve.wait_ge(loaded, all_loaded)
            for u in range(2):
                nc.vector.memset(q_bd[u][:], 0.0)
                nc.vector.memset(k_dense[u][QROWS:P], 1.0)
            nc.vector.memset(PV_BANK[:], 0.0)
            nc.vector.tensor_copy(ident_bf[:], ident[:])
            for i in range(2):
                t = nc.vector.tensor_copy(wqk_p[:, i], wqk_raw[:, i].rearrange("p (t j d) -> p j d t", j=QUADS, d=AE))
            t.then_inc(ready_dve, 1)
            dve.wait_ge(ready_dve, 1)
            dve.wait_ge(ready_pool, 1)

            def norm_stats(p):
                wait(dve, x_ln_in, (p + 1) * 16)
                layer_norm_stats(nc, dve, x_ln, bn, mv, n_half, n_seen, n_stat, p + 1)

            def norm_apply(p):
                wait(dve, x_turn, p)
                normalise(nc, dve, x_ln, xh, mv, rstd, n_root, p + 1, xh_done)

            def take_first_part(p, i):
                if i == 0:
                    wait(dve, part_done[1][2], p)
                else:
                    wait(dve, part_done[0][2], p + 1)
                wait(dve, part_done[i][0], p + 1)
                nc.vector.tensor_tensor(left[:], PREP[:], part[:, i, 0], ALU.subtract).then_inc(part_left[i], 1)

            def maxima(it, a, f):
                u, s, t = where(a)
                n = (it * SLOTS + a) * FILLS + f
                if t == 0 and f == 0:
                    wait(dve, m_left_done, it * 4 + (a // TILES - 1))
                wait(dve, a_mm, n + 1)
                q, j = f // 2, 2 * (f % 2)
                nc.vector.tensor_reduce(mx[s][:, q, t, j:j + 2], A_BANK[f % 2][:].rearrange("p (j k) -> p j k", j=2),
                                        AX.X, ALU.max).then_inc(a_max, 1)

            def attend_half(it, g):
                s, h, p = g % 2, it * 4 + g, it * 2 + g // 2
                c = slice(s * L, (s + 1) * L)
                wait(dve, pv_moved, (h + 1) * (16 * 2 * QUADS))
                nc.vector.reciprocal(att_r[:, c], att_d[:, c]).then_inc(sums_inv, 1)
                wait(dve, sums_inv, h + 1)
                wait(dve, o_mm, p)
                nc.vector.tensor_tensor(att[:, c], att_n[:, c], att_r[:, c], ALU.mult).then_inc(att_done, 1)

            def add_residual(p):
                wait(dve, o_mm, p + 1)
                wait(dve, x_res_in, (p + 1) * 16)
                wait(dve, o_turn, p)
                nc.vector.tensor_tensor(flat(o_s), TAIL[:], flat(x_res), ALU.add).then_inc(o_done, 1)

            def add_expert(p):
                wait(dve, f2_mm, p + 1)
                wait(dve, x_b2_done, p + 1)
                wait(dve, y_ready, p)
                nc.vector.tensor_tensor(flat(y_s), TAIL[:], flat(x_b2), ALU.add).then_inc(y_sum, 1)
                wait(dve, y_sum, p + 1)
                layer_norm_stats(nc, dve, y_s, bn2, mv2, n2_half, n2_seen, n2_stat, p + 1)

            def finish(p):
                wait(dve, stored, p * 16)
                normalise(nc, dve, y_s, y_out, mv2, rstd2, n2_root, p + 1, y_ready)

            def slots(it, last):
                for k in range(SLOTS):
                    a = FIRST + LEAD + k
                    for f in range(FILLS):
                        if not (last and a >= SLOTS):
                            maxima(it, a, f)
                        for u in range(2):
                            p = it * 2 + 2 + u
                            if not last:
                                if (k, f) == (LN_AT[u], 0):
                                    norm_stats(p)
                                if (k, f) == (LN_AT[u] + 1, 0):
                                    norm_apply(p)
                                for i, at in enumerate((Q_AT, K_AT)):
                                    if (k, f) == (at[u], 1):
                                        take_first_part(p, i)
                            p = it * 2 + u
                            if (k, f) == (O_AT[u], 1):
                                add_residual(p)
                            if (k, f) == (F2_AT[u], 3):
                                add_expert(p)
                            if k == F2_AT[u] + (1 - u) and f == 3:
                                finish(p)
                        if f == 3 and k in ATT_AT:
                            g = ATT_AT[k]
                            attend_half(it, g)

            for p in range(2):
                norm_stats(p)
                norm_apply(p)
                for i in range(2):
                    take_first_part(p, i)
            for T in range(-LEAD, FIRST):
                for f in range(FILLS):
                    maxima(0, T + LEAD, f)
            with dve.Fori(0, TURNS - 1) as it:
                slots(it, False)
            slots(TURNS - 1, True)


def build(nc, out, attn_in, ffn_in, c_xpos, c_mask, c_ident):
    with ExitStack() as ctx:
        bank = [ctx.enter_context(nc.psum_tensor(f"bank{i}", [P, 512], F32)) for i in range(8)]
        x1_all = ctx.enter_context(nc.sbuf_tensor("x1_all", [P, UNITS, NC, D], F32))
        used = retention_block(nc, bank, x1_all, *attn_in, c_xpos, c_mask, c_ident)
        nc.clear_and_free_semaphores(used)
        nc.all_engine_barrier()
        attention_block(nc, bank, x1_all, out, *ffn_in, c_ident)


def constants():
    import numpy as np

    pos = np.arange(L, dtype=np.float32)
    base = ((np.arange(0, RE, 2, dtype=np.float32) + np.float32(0.4 * RE)) / np.float32(1.4 * RE)).astype(np.float64)
    scale = base[None, :] ** (pos / np.float32(512.0)).astype(np.float64)[:, None]
    half = RE // 2
    inv = (1.0 / 10000.0 ** (np.arange(half) / half)).astype(np.float32)
    angle = (pos[:, None] * inv[None, :]).astype(np.float32).astype(np.float64)
    gamma = (1.0 - np.exp(np.linspace(np.log(1 / 32), np.log(1 / 64), RH))).astype(np.float32)
    log_gamma = np.log(gamma).astype(np.float32).astype(np.float64)
    decay = np.exp(log_gamma[:, None] * (np.arange(L) - L // 2)[None, :])
    out = np.zeros((4, RE, RH, L))
    for i, (s, dec) in enumerate(((scale, decay), (1.0 / scale, 1.0 / decay))):
        for e in range(RE):
            out[2 * i, e] = (np.cos(angle) * s)[:, e // 2][None, :] * dec
            out[2 * i + 1, e] = (np.sin(angle) * s)[:, e // 2][None, :] * dec
    xpos = out.reshape(4, P, L).transpose(1, 0, 2).astype(np.float32)
    mask = (np.arange(P)[:, None] <= np.arange(P)[None, :]).astype(np.float32)
    return {"c_xpos": np.ascontiguousarray(xpos), "c_mask": mask, "c_ident": np.eye(P, dtype=np.float32)}


_A = ["X", "Wq", "Wk", "Wv", "W_G", "W_O", "gn_w", "gn_b", "ln1_w", "ln1_b", "ln2_w", "ln2_b",
      "ffn_w1", "ffn_b1", "ffn_w2", "ffn_b2"]
_F = ["ln_g", "ln_b", "wq", "wk", "wv", "wo", "w1", "b1", "w2", "b2"]


def kernel(**inputs):
    import numpy as _np
    import concourse.bacc as _bacc
    from concourse.bass_utils import run_bass_kernel_spmd as _run
    nc = _bacc.Bacc("TRN2", target_bir_lowering=False, num_devices=1)
    arrays, args = {}, {}
    for name in ["L0_attn_" + s for s in _A] + ["L0_ffn_" + s for s in _F]:
        arrays[f"in_{name}"] = _np.ascontiguousarray(inputs[name])
    arrays.update(constants())
    for k, v in arrays.items():
        args[k] = nc.dram_tensor(k, v.shape, mybir.dt.from_np(v.dtype), kind="ExternalInput").ap()
    out = nc.dram_tensor("out_0_dram", (SEQS, L, D), F32, kind="ExternalOutput").ap()
    build(nc, out, [args[f"in_L0_attn_{s}"] for s in _A], [args[f"in_L0_ffn_{s}"] for s in _F],
          args["c_xpos"], args["c_mask"], args["c_ident"])
    r = _run(nc, [arrays], core_ids=[0])
    return r.results[0]["out_0_dram"]
```

```python
from contextlib import ExitStack

import concourse.bass as bass
from concourse import mybir

F32 = mybir.dt.float32
BF16 = mybir.dt.bfloat16
ALU = mybir.AluOpType
ACT = mybir.ActivationFunctionType
AX = mybir.AxisListType

P = 128
D = 128
FFN = 512
NF = FFN // P
LAYERS = 2
SEQS, L = 32, 256
UNIT = 512
NC = UNIT // P
SPU = UNIT // L
UNITS = SEQS // SPU
TURNS = UNITS // 2
EPS = 1e-5

PARTS = 3
Q_PART = (0, 0, 0, 1, 1, 2)
K_PART = (0, 1, 2, 0, 1, 0)
TERMS = len(Q_PART)

RH, RE = 8, 16
RROWS = TERMS * RE
HEADS = SPU * RH

AH, AE = 32, 4
QUADS = 4
TILES = AH // QUADS
EXPERTS = 8
VW = 2 * AE


def count(n):
    return max(n, 0) if isinstance(n, int) else n


def flat(t):
    return t.rearrange("p a b -> p (a b)")


def layer_norm_stats(nc, dve, src, bn, mv, halves_done, halves_seen, done, n):
    for c in range(NC):
        last = nc.vector.bn_stats(bn[:, c], src[:, c])
    last.then_inc(halves_done, 1)
    dve.wait_ge(halves_done, n)
    dve.sem_inc(halves_seen, 1)
    for c in range(NC):
        last = nc.vector.bn_aggr(mv[:, c], bn[:, c])
    last.then_inc(done, 1)


def inverse_root(nc, pool, mv, var, rstd, eps, minus_half, stats_done, var_done, done, n):
    pool.wait_ge(stats_done, n)
    nc.gpsimd.tensor_tensor(var[:], mv[:, :, 1], eps[:], ALU.add).then_inc(var_done, 1)
    pool.wait_ge(var_done, n)
    nc.gpsimd.tensor_tensor(rstd[:], var[:], minus_half[:], ALU.pow).then_inc(done, 1)


def normalise(nc, dve, src, dst, mv, rstd, rstd_done, n, done):
    dve.wait_ge(rstd_done, n)
    for c in range(NC):
        last = nc.vector.tensor_scalar(dst[:, c], src[:, c], mv[:, c, 0:1], rstd[:, c:c + 1],
                                       ALU.subtract, ALU.mult)
    last.then_inc(done, 1)


def retention_block(nc, bank, x1_all, X, Wq, Wk, Wv, W_G, W_O, gn_w, gn_b, ln1_w, ln1_b, ln2_w, ln2_b,
                    ffn_w1, ffn_b1, ffn_w2, ffn_b2, c_xpos, c_mask, c_ident):
    x_units = X.rearrange("(n s) (h p) d -> p n (s h) d", s=SPU, p=P)

    LOAD, NORM_1, ROOT_1, APPLY_1, TURN_1, SCALE_1 = 0, 2, 4, 5, 6, 7
    Q, K, V, G = 8, 10, 12, 12
    ROTATE, PART_0, LEAVE, PART_1, PART_2 = (9, 11), (11, 13), (11, 13), (12, 14), (13, 15)
    STACK, KEEP_V, TANH, GATE, GATES = 10, 13, 14, 15, 16
    EACH = 2
    HEAD_0, MASK_AFTER, PV_AFTER = 18, 0, 1
    GROUP = RH // 2
    GROUPS = HEADS // GROUP
    Y, TURN_Y, MEAN, SQUARE, GATED, VARIANCE, DEVIATION, Z = 27, 28, 29, 30, 30, 31, 31, 32
    TURN_Z, KEEP_Z, O, RES, ROOT_2, APPLY_2, TURN_2, SCALE_2 = 33, 34, 35, 36, 37, 38, 39, 41
    F1, GELU_AFTER, F2, SUM, STEPS = (42, 42, 42, 42), 0, (43, 44, 45, 46), 47, 48
    LAG = 4

    with ExitStack() as ctx:
        def sb(name, shape, dt=F32):
            return ctx.enter_context(nc.sbuf_tensor(name, shape, dt))

        def two(name, shape, dt=F32):
            return [sb(f"{name}{u}", shape, dt) for u in range(2)]

        used = []

        def sem(name):
            used.append(nc.alloc_semaphore(name))
            return used[-1]

        def sems(names):
            return [[sem(f"{n}_{u}") for u in range(2)] for n in names.split()]

        ident = sb("ident", [P, P])
        xpos = sb("xpos", [P, 4, L])
        mask = sb("mask", [P, P])
        minus_half = sb("minus_half", [P, NC])
        eps = sb("eps", [P, NC])
        wqk_raw = sb("wqk_raw", [P, LAYERS, 2, RH, RE])
        wqk = sb("wqk", [P, LAYERS, 4, RE, RH])
        wv_s = sb("wv_s", [P, LAYERS, RH, RE])
        wg_s = sb("wg_s", [P, LAYERS, D])
        wo_s = sb("wo_s", [P, LAYERS, D])
        w1_s = sb("w1_s", [P, LAYERS, FFN])
        w2_s = sb("w2_s", [P, LAYERS, NF, D])
        b1_s = sb("b1_s", [P, LAYERS, NF])
        b2_s = sb("b2_s", [P, LAYERS, D])
        gnw_s = sb("gnw_s", [P, LAYERS, D])
        gnb_s = sb("gnb_s", [P, LAYERS, D])
        ln_s = sb("ln_s", [P, 4, LAYERS])

        xin = two("xin", [P, NC, D])
        res = two("res", [P, NC, D])
        resb = two("resb", [P, NC, D])
        bn = two("bn", [P, NC, 6])
        mv = two("mv", [P, NC, 2])
        var = two("var", [P, NC])
        rstd = two("rstd", [P, NC])
        xh = two("xh", [P, NC, D])
        hT = two("hT", [P, UNIT])
        rot_a = two("rot_a", [P, UNIT])
        rot_b = two("rot_b", [P, UNIT])
        qk = two("qk", [P, 2, UNIT])
        part = two("part", [P, 2, PARTS, UNIT], BF16)
        stack = two("stack", [P, RH, 2, UNIT], BF16)
        v_pad = two("v_pad", [P, NC, RH, 2 * RE])
        gate_t = two("gate_t", [P, UNIT])
        gate = two("gate", [P, NC, D])
        gate_w = two("gate_w", [P, NC, D])
        gate_b = two("gate_b", [P, NC, D])
        PB = 2 * GROUP
        scratch = two("scratch", [P, PB * 3 * P])
        prob = [[scratch[u][:, i * 3 * P:(i + 1) * 3 * P].rearrange("p (a b) -> p a b", b=P) for i in range(PB)]
                for u in range(2)]
        hidden = [scratch[u][:, 0:NF * UNIT].rearrange("p (f t) -> p f t", t=UNIT) for u in range(2)]
        y = two("y", [P, UNIT])
        g_sum = two("g_sum", [P, NC * RH])
        g_stat = two("g_stat", [P, NC * RH])
        dev = two("dev", [P, NC, D])
        zT = two("zT", [P, UNIT])

        sp_seen = sem("sp_seen")
        loaded, turned_w, padded = sem("weights_loaded"), sem("weights_turned"), sem("v_pad_zeroed")
        x_in, x_summed, x1_ready, x1_stored = sems("x_in x_summed x1_ready x1_stored")
        n_half, n_seen, n_stat, n_var, n_root = sems("n_half n_seen n_stat n_var n_root")
        n1_done, n1_turn, n1_hT = sems("n1_done n1_turn n1_hT")
        n2_done, n2_turn, n2_hT = sems("n2_done n2_turn n2_hT")
        q_mm, qt_mm, k_mm, kt_mm, v_mm, g_mm = sems("q_mm qt_mm k_mm kt_mm v_mm g_mm")
        mm_of = ((q_mm, qt_mm), (k_mm, kt_mm))
        rotated, full = sems("q_rotated k_rotated"), sems("q_full k_full")
        part_done = [sems(f"{q}_part0 {q}_part1 {q}_part2") for q in "qk"]
        part_left = sems("q_left k_left")
        stacked, = sems("stacked")
        v_ready, tanh_done, gate_done, gates_done = sems("v_ready tanh_done gate_done gates_done")
        s_mm, s_off, s_masked, pv_mm = sems("s_mm s_off s_masked pv_mm")
        y_done, y_turn = sems("y_done y_turn")
        g_sum_done, g_dev, g_gated, g_sq, g_sqsum, g_sd, g_root, g_norm, z_done = sems(
            "g_sum_done g_dev g_gated g_sq g_sqsum g_sd g_root g_norm z_done")
        z_turn, zT_done, o_mm, o_res, resb_done, f2_mm, f_res = sems(
            "z_turn zT_done o_mm o_res resb_done f2_mm f_res")
        f1_mm = sems("f1_mm0 f1_mm1 f1_mm2 f1_mm3")
        gelu_done = sems("gelu0 gelu1 gelu2 gelu3")

        def B(u, i):
            return bank[4 * u + i]

        def norm_count(it, l, second=0):
            return it * (2 * LAYERS + 1) + (2 * l + second + 1)

        def chunk(t, c):
            return t[:, c * P:(c + 1) * P]

        def head_at(j):
            return 2 * (j % GROUP) + j // GROUP % 2

        def head(s, after=0):
            i = s - HEAD_0 - after
            return range(i * EACH, (i + 1) * EACH) if 0 <= i < HEADS // EACH else range(0)

        F_BANK = (2, 3, 0, 1)
        S_BANK = (3, 0)

        loads = [(ident[:], c_ident), (xpos[:], c_xpos), (mask[:], c_mask)]
        for l in range(LAYERS):
            loads += [(wqk_raw[:, l, 0], Wq[l].rearrange("h d e -> d h e")),
                      (wqk_raw[:, l, 1], Wk[l].rearrange("h d e -> d h e")),
                      (wv_s[:, l], Wv[l].rearrange("h d e -> d h e")),
                      (wg_s[:, l], W_G[l]), (wo_s[:, l], W_O[l]), (w1_s[:, l], ffn_w1[l]),
                      (w2_s[:, l], ffn_w2[l].rearrange("(f p) n -> p f n", p=P)),
                      (b1_s[:, l], ffn_b1[l].rearrange("(f p) -> p f", p=P)),
                      (b2_s[:, l], ffn_b2[l:l + 1, :].to_broadcast([P, D])),
                      (gnw_s[:, l], gn_w[l:l + 1, :].to_broadcast([P, D])),
                      (gnb_s[:, l], gn_b[l:l + 1, :].to_broadcast([P, D]))]
            loads += [(ln_s[:, i, l:l + 1], v[l].rearrange("(p a) -> p a", a=1))
                      for i, v in enumerate((ln1_w, ln1_b, ln2_w, ln2_b))]
        all_loaded = 16 * len(loads)

        block = ctx.enter_context(nc.Block())

        def steps(step, it, last):
            for t in range(LAYERS * STEPS):
                for u in (0, 1):
                    at = t + (1 - u) * LAG
                    if at < LAYERS * STEPS:
                        step(u, it, at // STEPS, at % STEPS)
                    elif not last:
                        step(u, it + 1, at // STEPS - LAYERS, at % STEPS)

        def run(eng, step):
            for t in range(LAG):
                step(0, 0, 0, t)
            with eng.Fori(0, TURNS - 1) as it:
                steps(step, it, False)
            steps(step, TURNS - 1, True)

        @block.sync
        def _(sp):
            for dst, src in loads:
                with nc.allow_non_contiguous_dma("weights, once"):
                    sp.dma_start(dst, src).then_inc(loaded, 16)

            def stack_parts(u, n):
                sp.wait_ge(pv_mm[u], (n - 1) * GROUPS)
                sp.sem_inc(sp_seen, 1)
                ready = [-1, -1]
                for t in range(TERMS):
                    for i, p in enumerate((Q_PART[t], K_PART[t])):
                        if p > ready[i]:
                            sp.wait_ge(part_done[i][p][u], n)
                            sp.sem_inc(sp_seen, 1)
                            ready[i] = p
                    q, k = Q_PART[t], PARTS + K_PART[t]
                    src = part[u][:].rearrange("p i c t -> p (i c) t")[:, q:k + 1:k - q]
                    sp.dma_start(stack[u][t * RE:(t + 1) * RE], src).then_inc(stacked[u], 16)

            def load_x(u, it):
                p, turn = sp.snap(it * 2 + u), sp.snap(it * 1)
                sp.wait_ge(x_summed[u], turn)
                sp.dma_start(xin[u][:].unsqueeze(1), x_units[:, bass.ds(p, 1)]).then_inc(x_in[u], 16)

            def step(u, it, l, s):
                n = sp.snap(it * LAYERS + (l + 1))
                if (l, s) == (0, LOAD):
                    load_x(u, it)
                if s == STACK:
                    stack_parts(u, n)
                if (l, s) == (LAYERS - 1, SUM):
                    p, turn = sp.snap(it * 2 + u), sp.snap(it + 1)
                    sp.wait_ge(x1_ready[u], turn)
                    sp.dma_start(x1_all[:, bass.ds(p, 1)], xh[u][:].unsqueeze(1)).then_inc(x1_stored[u], 16)

            run(sp, step)
            for u in range(2):
                sp.wait_ge(x1_stored[u], 16 * TURNS)

        @block.tensor
        def _(pe):
            pe.wait_ge(loaded, all_loaded)
            pe.wait_ge(turned_w, 1)

            def scores(u, n, j):
                s, h = j // RH, head_at(j)
                if j >= 2:
                    pe.wait_ge(s_masked[u], (n - 1) * HEADS + (j - 1))
                b = B(u, S_BANK[j % 2])
                t0 = s * L
                nc.tensor.matmul(b[:, 0:L], stack[u][0:RROWS, h, 1, t0:t0 + P],
                                 stack[u][0:RROWS, h, 0, t0:t0 + L], start=True, stop=True)
                nc.tensor.matmul(b[:, L:L + P], stack[u][0:RROWS, h, 1, t0 + P:t0 + L],
                                 stack[u][0:RROWS, h, 0, t0 + P:t0 + L], start=True, stop=True
                                 ).then_inc(s_mm[u], 1)

            def times_v(u, n, g):
                s, odd = g // 2, g % 2
                pe.wait_ge(s_masked[u], (n - 1) * HEADS + (g + 1) * GROUP)
                o = [B(u, 1)[32 * i:32 * (i + 1), s * L:(s + 1) * L] for i in range(GROUP)]
                p = [prob[u][(g * GROUP + i) % PB] for i in range(GROUP)]
                for i in range(GROUP):
                    nc.tensor.matmul(o[i], v_pad[u][:, 2 * s, 2 * i + odd], flat(p[i][:, 0:2]),
                                     start=(odd == 0), stop=False, skip_group_check=True)
                for i in range(GROUP):
                    t = nc.tensor.matmul(o[i][:, P:L], v_pad[u][:, 2 * s + 1, 2 * i + odd], p[i][:, 2],
                                         start=False, stop=(odd == 1), skip_group_check=True)
                t.then_inc(pv_mm[u], 1)

            def step(u, it, l, s):
                n = it * LAYERS + (l + 1)
                if s == TURN_1:
                    pe.wait_ge(n1_done[u], n)
                    for c in range(NC):
                        t = nc.tensor.transpose(chunk(B(u, 0), c), xh[u][:, c], ident[:])
                    t.then_inc(n1_turn[u], 1)
                if s in (Q, K):
                    pe.wait_ge(n1_hT[u], n)
                    for i, b, done in (((0, 1, q_mm), (1, 2, qt_mm)) if s == Q else ((2, 3, k_mm), (3, 0, kt_mm))):
                        nc.tensor.matmul(B(u, b)[:], flat(wqk[:, l, i]), hT[u][:], start=True, stop=True
                                         ).then_inc(done[u], 1)
                if s == V:
                    pe.wait_ge(rotated[0][u], n)
                    for c in range(NC):
                        t = nc.tensor.matmul(chunk(B(u, 1), c), chunk(hT[u], c), flat(wv_s[:, l]),
                                             start=True, stop=True)
                    t.then_inc(v_mm[u], 1)
                if s == G:
                    for c in range(NC):
                        t = nc.tensor.matmul(chunk(B(u, 2), c), chunk(hT[u], c), wg_s[:, l],
                                             start=True, stop=True)
                    t.then_inc(g_mm[u], 1)
                if s == HEAD_0:
                    pe.wait_ge(stacked[u], n * (16 * TERMS))
                    pe.wait_ge(rotated[1][u], n)
                    pe.wait_ge(v_ready[u], n)
                for j in head(s):
                    scores(u, n, j)
                for j in head(s, PV_AFTER):
                    if j % GROUP == GROUP - 1:
                        times_v(u, n, j // GROUP)
                if s == TURN_Y:
                    pe.wait_ge(y_done[u], n)
                    pe.wait_ge(gate_done[u], n)
                    for c in range(NC):
                        t = nc.tensor.transpose(chunk(B(u, 2), c), chunk(y[u], c), ident[:])
                    t.then_inc(y_turn[u], 1)
                if s == TURN_Z:
                    pe.wait_ge(z_done[u], n)
                    for c in range(NC):
                        t = nc.tensor.transpose(chunk(B(u, 3), c), dev[u][:, c], ident[:])
                    t.then_inc(z_turn[u], 1)
                if s == O:
                    pe.wait_ge(zT_done[u], n)
                    for c in range(NC):
                        t = nc.tensor.matmul(chunk(B(u, 0), c), chunk(zT[u], c), wo_s[:, l],
                                             start=True, stop=True)
                    t.then_inc(o_mm[u], 1)
                if s == TURN_2:
                    pe.wait_ge(n2_done[u], n)
                    for c in range(NC):
                        t = nc.tensor.transpose(chunk(B(u, 1), c), xh[u][:, c], ident[:])
                    t.then_inc(n2_turn[u], 1)
                for f in range(NF):
                    if s == F1[f]:
                        pe.wait_ge(n2_hT[u], n)
                        nc.tensor.matmul(B(u, F_BANK[f])[:], w1_s[:, l, f * P:(f + 1) * P], hT[u][:],
                                         start=True, stop=True).then_inc(f1_mm[f][u], 1)
                for c in range(NC):
                    if s == F2[c]:
                        for f in range(NF):
                            if c == 0:
                                pe.wait_ge(gelu_done[f][u], n)
                            t = nc.tensor.matmul(chunk(B(u, 2), c), chunk(hidden[u][:, f], c), w2_s[:, l, f],
                                                 start=(f == 0), stop=(f == NF - 1))
                        if c == NC - 1:
                            t.then_inc(f2_mm[u], 1)

            run(pe, step)

        @block.scalar
        def _(act):
            act.wait_ge(loaded, all_loaded)
            act.wait_ge(padded, 1)

            def step(u, it, l, s):
                n = it * LAYERS + (l + 1)
                if s == SCALE_1:
                    act.wait_ge(n1_turn[u], n)
                    nc.scalar.activation(hT[u][:], B(u, 0)[:], ACT.Identity, scale=ln_s[:, 0, l:l + 1],
                                         bias=ln_s[:, 1, l:l + 1]).then_inc(n1_hT[u], 1)
                for i in range(2):
                    if s == PART_0[i]:
                        act.wait_ge(stacked[u], (n - 1) * (16 * TERMS))
                        act.wait_ge(full[i][u], n)
                        nc.scalar.activation(part[u][:, i, 0], qk[u][:, i], ACT.Copy
                                             ).then_inc(part_done[i][0][u], 1)
                    if s == PART_1[i]:
                        act.wait_ge(part_left[i][u], n)
                        nc.scalar.activation(part[u][:, i, 1], qk[u][:, i], ACT.Copy
                                             ).then_inc(part_done[i][1][u], 1)
                if s == KEEP_V:
                    act.wait_ge(v_mm[u], n)
                    v = B(u, 1)[:].rearrange("p (c r o e) -> p c r o e", c=NC, o=2, e=RE)
                    for odd in range(2):
                        a = nc.scalar.activation(v_pad[u][:, :, odd::2, odd * RE:(odd + 1) * RE], v[:, :, :, odd],
                                                 ACT.Copy)
                    a.then_inc(v_ready[u], 1)
                if s == TANH:
                    act.wait_ge(g_mm[u], n)
                    nc.scalar.activation(gate_t[u][:], B(u, 2)[:], ACT.Tanh, scale=0.5).then_inc(tanh_done[u], 1)
                for j in head(s):
                    act.wait_ge(s_mm[u], (n - 1) * HEADS + (j + 1))
                    act.wait_ge(pv_mm[u], (n - 1) * GROUPS + max(j // GROUP - PB // GROUP + 1, 0))
                    nc.scalar.activation(prob[u][j % PB][:, 1], B(u, S_BANK[j % 2])[:, P:L], ACT.Copy
                                         ).then_inc(s_off[u], 1)
                if s == Y:
                    act.wait_ge(pv_mm[u], n * GROUPS)
                    nc.scalar.activation(y[u][:], B(u, 1)[:], ACT.Copy).then_inc(y_done[u], 1)
                if s == SQUARE:
                    act.wait_ge(g_dev[u], n)
                    nc.scalar.activation(gate_t[u][:], flat(dev[u]), ACT.Square).then_inc(g_sq[u], 1)
                if s == DEVIATION:
                    act.wait_ge(g_sqsum[u], n)
                    nc.scalar.activation(g_stat[u][:], g_sum[u][:], ACT.Sqrt, scale=1.0 / RE, bias=eps[:, 0:1]
                                         ).then_inc(g_sd[u], 1)
                if s == KEEP_Z:
                    act.wait_ge(z_turn[u], n)
                    nc.scalar.activation(zT[u][:], B(u, 3)[:], ACT.Copy).then_inc(zT_done[u], 1)
                if s == SCALE_2:
                    act.wait_ge(n2_turn[u], n)
                    nc.scalar.activation(hT[u][:], B(u, 1)[:], ACT.Identity, scale=ln_s[:, 2, l:l + 1],
                                         bias=ln_s[:, 3, l:l + 1]).then_inc(n2_hT[u], 1)
                for f in range(NF):
                    if s == F1[f] + GELU_AFTER:
                        act.wait_ge(f1_mm[f][u], n)
                        nc.scalar.activation(hidden[u][:, f], B(u, F_BANK[f])[:], ACT.Gelu,
                                             bias=b1_s[:, l, f:f + 1]).then_inc(gelu_done[f][u], 1)

            run(act, step)

        @block.gpsimd
        def _(pool):
            nc.gpsimd.memset(minus_half[:], -0.5)
            nc.gpsimd.memset(eps[:], EPS)
            for u in range(2):
                t = nc.gpsimd.memset(v_pad[u][:], 0.0)
            t.then_inc(padded, 1)
            pool.wait_ge(padded, 1)
            pool.wait_ge(loaded, all_loaded)
            pool.wait_ge(turned_w, 1)

            def root(u, n):
                inverse_root(nc, pool, mv[u], var[u], rstd[u], eps, minus_half, n_stat[u], n_var[u], n_root[u], n)

            def step(u, it, l, s):
                n = it * LAYERS + (l + 1)
                if s == ROOT_1:
                    root(u, norm_count(it, l))
                for i in range(2):
                    if s == PART_2[i]:
                        pool.wait_ge(part_done[i][1][u], n)
                        nc.gpsimd.tensor_tensor(part[u][:, i, 2], qk[u][:, i], part[u][:, i, 1], ALU.subtract
                                                ).then_inc(part_done[i][2][u], 1)
                if s == GATES:
                    pool.wait_ge(gate_done[u], n)
                    nc.gpsimd.tensor_tensor(gate_w[u][:], gate[u][:],
                                            gnw_s[:, l].unsqueeze(1).to_broadcast([P, NC, D]), ALU.mult)
                    nc.gpsimd.tensor_tensor(gate_b[u][:], gate[u][:],
                                            gnb_s[:, l].unsqueeze(1).to_broadcast([P, NC, D]), ALU.mult
                                            ).then_inc(gates_done[u], 1)
                if s == GATED:
                    pool.wait_ge(g_dev[u], n)
                    pool.wait_ge(gates_done[u], n)
                    nc.gpsimd.tensor_tensor(y[u][:], flat(dev[u]), flat(gate_w[u]), ALU.mult).then_inc(g_gated[u], 1)
                if s == ROOT_2:
                    root(u, norm_count(it, l, 1))
                    nc.gpsimd.tensor_tensor(resb[u][:], res[u][:],
                                            b2_s[:, l].unsqueeze(1).to_broadcast([P, NC, D]), ALU.add
                                            ).then_inc(resb_done[u], 1)
                if (l, s) == (LAYERS - 1, SUM):
                    root(u, norm_count(it, LAYERS))

            run(pool, step)

        @block.vector
        def _(dve):
            dve.wait_ge(loaded, all_loaded)
            for l in range(LAYERS):
                for i in range(2):
                    src = wqk_raw[:, l, i].rearrange("p h e -> p e h")
                    nc.vector.tensor_copy(wqk[:, l, 2 * i], src)
                    nc.vector.tensor_scalar(wqk[:, l, 2 * i + 1, 0::2], src[:, 1::2], -1.0, None, ALU.mult)
                    t = nc.vector.tensor_copy(wqk[:, l, 2 * i + 1, 1::2], src[:, 0::2])
            nc.vector.tensor_scalar(gnw_s[:], gnw_s[:], -0.5, None, ALU.mult)
            t = nc.vector.tensor_scalar(gnb_s[:], gnb_s[:], 0.5, None, ALU.mult)
            t.then_inc(turned_w, 1)

            def by_seq(t):
                return t.rearrange("p (s t) -> p s t", s=SPU)

            def by_head(t):
                return t.rearrange("p (g e) -> p g e", e=RE)

            def per_head(t):
                return t[:].unsqueeze(2).to_broadcast([P, NC * RH, RE])

            def stats(u, src, n):
                layer_norm_stats(nc, dve, src[u], bn[u], mv[u], n_half[u], n_seen[u], n_stat[u], n)

            def rotate(u, n, i):
                cos = xpos[:, 2 * i].unsqueeze(1).to_broadcast([P, SPU, L])
                sin = xpos[:, 2 * i + 1].unsqueeze(1).to_broadcast([P, SPU, L])
                if i == 1:
                    dve.wait_ge(full[0][u], n)
                dve.wait_ge(mm_of[i][0][u], n)
                nc.vector.tensor_tensor(by_seq(rot_a[u][:]), by_seq(B(u, (1, 3)[i])[:]), cos, ALU.mult)
                dve.wait_ge(mm_of[i][1][u], n)
                nc.vector.tensor_tensor(by_seq(rot_b[u][:]), by_seq(B(u, (2, 0)[i])[:]), sin, ALU.mult
                                        ).then_inc(rotated[i][u], 1)
                dve.wait_ge(rotated[i][u], n)
                nc.vector.tensor_tensor(qk[u][:, i], rot_a[u][:], rot_b[u][:], ALU.add).then_inc(full[i][u], 1)

            def leave(u, n, i):
                dve.wait_ge(part_done[i][0][u], n)
                nc.vector.tensor_tensor(qk[u][:, i], qk[u][:, i], part[u][:, i, 0], ALU.subtract
                                        ).then_inc(part_left[i][u], 1)

            def step(u, it, l, s):
                n = it * LAYERS + (l + 1)
                src = xin if l == 0 else res
                if s == NORM_1:
                    if l == 0:
                        dve.wait_ge(x_in[u], (it + 1) * 16)
                    else:
                        dve.wait_ge(f_res[u], count(n - 1))
                    stats(u, src, norm_count(it, l))
                if s == APPLY_1:
                    if l == 0:
                        dve.wait_ge(x1_stored[u], it * 16)
                    normalise(nc, dve, src[u], xh[u], mv[u], rstd[u], n_root[u], norm_count(it, l), n1_done[u])
                for i in range(2):
                    if s == ROTATE[i]:
                        rotate(u, n, i)
                    if s == LEAVE[i]:
                        leave(u, n, i)
                if s == GATE:
                    dve.wait_ge(tanh_done[u], n)
                    nc.vector.scalar_tensor_tensor(flat(gate[u]), gate_t[u][:], 1.0, B(u, 2)[:], ALU.add, ALU.mult
                                                   ).then_inc(gate_done[u], 1)
                for j in head(s, MASK_AFTER):
                    dve.wait_ge(s_off[u], (n - 1) * HEADS + (j + 1))
                    b = B(u, S_BANK[j % 2])[:, 0:3 * P].rearrange("p (a b) -> p a b", b=P)
                    nc.vector.tensor_tensor(prob[u][j % PB][:, 0::2], b[:, 0::2],
                                            mask[:].unsqueeze(1).to_broadcast([P, 2, P]), ALU.mult
                                            ).then_inc(s_masked[u], 1)
                if s == MEAN:
                    dve.wait_ge(y_turn[u], n)
                    nc.vector.tensor_reduce(g_sum[u][:], by_head(B(u, 2)[:]), AX.X, ALU.add
                                            ).then_inc(g_sum_done[u], 1)
                    dve.wait_ge(g_sum_done[u], n)
                    nc.vector.scalar_tensor_tensor(by_head(flat(dev[u])), per_head(g_sum[u]), 1.0 / RE,
                                                   by_head(B(u, 2)[:]), ALU.mult, ALU.subtract
                                                   ).then_inc(g_dev[u], 1)
                if s == VARIANCE:
                    dve.wait_ge(g_sq[u], n)
                    nc.vector.tensor_reduce(g_sum[u][:], by_head(gate_t[u][:]), AX.X, ALU.add
                                            ).then_inc(g_sqsum[u], 1)
                if s == Z:
                    dve.wait_ge(g_sd[u], n)
                    nc.vector.reciprocal(g_stat[u][:], g_stat[u][:]).then_inc(g_root[u], 1)
                    dve.wait_ge(g_root[u], n)
                    dve.wait_ge(g_gated[u], n)
                    nc.vector.tensor_tensor(by_head(flat(dev[u])), by_head(y[u][:]), per_head(g_stat[u]), ALU.mult
                                            ).then_inc(g_norm[u], 1)
                    dve.wait_ge(g_norm[u], n)
                    nc.vector.tensor_tensor(flat(dev[u]), flat(dev[u]), flat(gate_b[u]), ALU.add).then_inc(z_done[u], 1)
                if s == RES:
                    dve.wait_ge(o_mm[u], n)
                    nc.vector.tensor_tensor(flat(res[u]), B(u, 0)[:], flat(src[u]), ALU.add).then_inc(o_res[u], 1)
                    dve.wait_ge(o_res[u], n)
                    stats(u, res, norm_count(it, l, 1))
                if s == APPLY_2:
                    normalise(nc, dve, res[u], xh[u], mv[u], rstd[u], n_root[u], norm_count(it, l, 1), n2_done[u])
                if s == F2[-1]:
                    dve.wait_ge(f2_mm[u], n)
                    dve.wait_ge(resb_done[u], n)
                    nc.vector.tensor_tensor(flat(res[u]), B(u, 2)[:], flat(resb[u]), ALU.add).then_inc(f_res[u], 1)
                if (l, s) == (LAYERS - 1, SUM):
                    dve.wait_ge(f_res[u], (it + 1) * LAYERS)
                    nc.vector.tensor_tensor(resb[u][:], res[u][:], xin[u][:], ALU.add).then_inc(x_summed[u], 1)
                    dve.wait_ge(x_summed[u], it + 1)
                    stats(u, resb, norm_count(it, LAYERS))
                if (l, s) == (LAYERS - 1, SUM):
                    normalise(nc, dve, resb[u], xh[u], mv[u], rstd[u], n_root[u], norm_count(it, LAYERS), x1_ready[u])

            run(dve, step)
    return used


def attention_block(nc, bank, x1_all, terms, out, ln_g, ln_b, wq, wk, wv, wo, w1, b1, w2, b2, c_ident):
    out_units = out.rearrange("(n s) (h p) d -> p n (s h) d", s=SPU, p=P)
    SLOTS = 2 * SPU * TILES
    FIRST, LEAD = 11, 11
    FILLS = 4
    PAIR_TILES = SPU * TILES
    QROWS = AE * TERMS * QUADS
    LN_AT, TURN_AT, Q_AT, K_AT, V_AT = (1, 13), (3, 16), (4, 17), (5, 18), (6, 23)
    Q_TERMS_AT, K_TERMS_AT, READ_AT = (5, 18), (6, 19), (6, 22)
    ATTEND_AT, O_AT, OT_AT, F1_AT, F2_AT, OUT_AT = (9, 25), (11, 26), (12, 27), (13, 28), (14, 29), (15, 30)
    COLLECT_AT = {0: 0, 6: 1, 14: 2, 21: 3}
    PV_FILLS, PV_OUT_FILL = (0, 1), 2
    GELU_FILL = 0
    EVEN_AT = (2, 20)
    MAX_AT = {3: 2, 11: 3, 19: 4, 27: 5}
    COLLECT_AT = {0: 0, 6: 1, 14: 2, 21: 3}
    SPREAD_WRITES, SPREAD_READS = 6, 2 * QUADS

    with ExitStack() as ctx:
        def sb(name, shape, dt=F32):
            return ctx.enter_context(nc.sbuf_tensor(name, shape, dt))

        def two(name, shape, dt=F32):
            return [sb(f"{name}{u}", shape, dt) for u in range(2)]

        sem = nc.alloc_semaphore

        ident = sb("a_ident", [P, P])
        ident_bf = sb("a_ident_bf", [P, P], BF16)
        minus_half, eps = sb("a_minus_half", [P, NC]), sb("a_eps", [P, NC])
        minus_one, zero = sb("minus_one", [P, 2, QUADS, TILES]), sb("zero", [P, 2, QUADS, TILES])
        g_s = sb("g_s", [P, 2])
        wqk_raw = sb("a_wqk_raw", [P, 2, D])
        wqk_p = sb("wqk_p", [P, 2, QUADS, AE, TILES])
        wv_s = sb("a_wv", [P, D])
        wo_p = sb("wo_p", [P, D])
        w1_s, w2_s = two("a_w1", [P, FFN]), two("a_w2", [P, NF, D])
        b1_s, b2_s = two("a_b1", [P, NF]), two("a_b2", [P, D])

        x_ln = sb("x_ln", [P, NC, D])
        bn, mv, var, rstd = sb("a_bn", [P, NC, 6]), sb("a_mv", [P, NC, 2]), sb("a_var", [P, NC]), sb("a_rstd", [P, NC])
        xh = sb("a_xh", [P, NC, D])
        hT = sb("a_hT", [P, UNIT])
        left = sb("left", [P, UNIT])
        part = sb("a_part", [P, 2, PARTS, UNIT], BF16)
        q_bd = two("q_bd", [P, QUADS, TILES, UNIT], BF16)
        k_dense = two("k_dense", [P, TILES, UNIT], BF16)
        v_ones = two("v_ones", [P, NC, AH, VW])
        mx = two("mx", [P, 2, TILES, QUADS])
        m_neg, m_left = sb("m_neg", [P, 2, QUADS, TILES]), sb("m_left", [P, 2, QUADS, TILES])
        m_part = sb("m_part", [P, 2, P], BF16)
        mT = sb("mT", [P, L], BF16)
        prob = two("a_prob", [P, 2, QUADS, L])
        pv_s = two("pv_s", [P, TILES, L])
        att_n, att_d = sb("att_n", [P, UNIT]), sb("att_d", [P, UNIT])
        att = sb("att", [P, UNIT])
        x_res, x_b2 = sb("x_res", [P, NC, D]), sb("x_b2", [P, NC, D])
        o_s, oT = sb("o_s", [P, NC, D]), sb("oT", [P, UNIT])
        hidden = sb("a_hidden", [P, NF, UNIT])
        y_s = sb("y_s", [P, NC, D])
        bn2, mv2, var2, rstd2 = (sb("a_bn2", [P, NC, 6]), sb("a_mv2", [P, NC, 2]), sb("a_var2", [P, NC]),
                                 sb("a_rstd2", [P, NC]))

        loaded, wo_in, cleared, ready_dve, ready_pool = map(sem, (
            "a_loaded", "wo_in", "cleared", "a_ready_dve", "a_ready_pool"))
        x_ln_in, n_half, n_seen, n_stat, n_var, n_root, xh_done = map(sem, (
            "x_ln_in", "an_half", "an_seen", "an_stat", "an_var", "an_root", "xh_done"))
        x_turn, hT_done = sem("x_turn"), sem("hT_done")
        qk_mm = [sem("aq_mm"), sem("ak_mm")]
        part_done = [[sem(f"a{q}_part{i}") for i in range(PARTS)] for q in "qk"]
        part_left = [sem("aq_left"), sem("ak_left")]
        terms_out, stacked = sem("terms_out"), sem("a_stacked")
        v_mm, v_ready = sem("av_mm"), sem("av_ready")
        a_mm, a_max, b_mm, b_exp, pv_mm, pv_out, pv_moved = map(sem, (
            "a_mm", "a_max", "b_mm", "b_exp", "apv_mm", "pv_out", "pv_moved"))
        m_neg_done, m_part0, m_left_done, m_part1, m_part2, m_turn, mT_done, m_in = map(sem, (
            "m_neg_done", "m_part0", "m_left_done", "m_part1", "m_part2", "m_turn", "mT_done", "m_in"))
        sums_inv, att_done, o_mm, x_res_in, o_done, o_turn, oT_done = map(sem, (
            "sums_inv", "att_done", "ao_mm", "x_res_in", "o_done", "o_turn", "oT_done"))
        w_in, f1_mm, gelu, f2_mm, x_b2_done, y_sum = map(sem, (
            "w_in", "af1_mm", "a_gelu", "af2_mm", "x_b2_done", "y_sum"))
        n2_half, n2_seen, n2_stat, n2_var, n2_root, y_ready, stored, sp_seen, pool_seen = map(sem, (
            "n2_half", "n2_seen", "n2_stat", "n2_var", "n2_root", "y_ready", "stored", "a_sp_seen", "a_pool_seen"))
        W_DMAS = 4

        def chunk(t, c):
            return t[:, c * P:(c + 1) * P]

        def where(T):
            return (T // PAIR_TILES) % 2, (T // TILES) % SPU, T % TILES

        def b_bank(n):
            return (n - FIRST * FILLS) % 3

        A_BANK = bank[0:2]
        B_BANK = bank[2:5]
        PV_BANK, PREP, TAIL = bank[5], bank[6], bank[7]

        loads = [(ident[:], c_ident), (wqk_raw[:, 0], wq), (wqk_raw[:, 1], wk), (wv_s[:], wv),
                 (g_s[:, 0:1], ln_g.rearrange("(p a) -> p a", a=1)), (g_s[:, 1:2], ln_b.rearrange("(p a) -> p a", a=1))]
        wo_loads = []
        wo_rows = wo.rearrange("(t j d) n -> j d t n", j=QUADS, d=AE)
        for j in range(QUADS):
            for d in range(AE):
                r = (j * AE + d) * TILES
                wo_loads.append((wo_p[r:r + TILES], wo_rows[j, d]))
        all_loaded = 16 * len(loads)

        block = ctx.enter_context(nc.Block())

        @block.sync
        def _(sp):
            for dst, src in loads:
                with nc.allow_non_contiguous_dma("weights, once"):
                    sp.dma_start(dst, src).then_inc(loaded, 16)

            def load_x_ln(p):
                p, n = sp.snap(p), sp.snap(p * 1)
                sp.wait_ge(xh_done, n)
                sp.dma_start(x_ln[:].unsqueeze(1), x1_all[:, bass.ds(p, 1)]).then_inc(x_ln_in, 16)

            def load_x_res(p):
                p, n = sp.snap(p), sp.snap(p * 1)
                sp.wait_ge(o_done, n)
                sp.sem_inc(sp_seen, 1)
                sp.wait_ge(x_b2_done, n)
                sp.dma_start(x_res[:].unsqueeze(1), x1_all[:, bass.ds(p, 1)]).then_inc(x_res_in, 16)

            def load_expert(p, e, u):
                e = sp.snap(e)
                if u == 1 or not isinstance(p, int):
                    sp.wait_ge(f2_mm, count(p - 1))
                    sp.sem_inc(sp_seen, 1)
                    sp.wait_ge(x_b2_done, count(p - 1))
                    sp.sem_inc(sp_seen, 1)
                with nc.allow_non_contiguous_dma("bias by feature"):
                    sp.dma_start(w1_s[u][:].unsqueeze(1), w1.rearrange("e p n -> p e n")[:, bass.ds(e, 1)]
                                 ).then_inc(w_in, 16)
                    sp.dma_start(w2_s[u][:].unsqueeze(1), w2.rearrange("e (f p) n -> p e f n", p=P)[:, bass.ds(e, 1)]
                                 ).then_inc(w_in, 16)
                    sp.dma_start(b1_s[u][:].unsqueeze(1), b1.rearrange("e (f p) -> p e f", p=P)[:, bass.ds(e, 1)]
                                 ).then_inc(w_in, 16)
                    sp.dma_start(b2_s[u][:], b2[bass.ds(e, 1)].to_broadcast([P, D])).then_inc(w_in, 16)

            def write_terms(p, i):
                if i == 0:
                    sp.wait_ge(stacked, p * (16 * SPREAD_READS))
                    sp.sem_inc(sp_seen, 1)
                part_of, seen = (Q_PART, K_PART)[i], -1
                for c0, c1 in ((0, 3), (3, 5), (5, 6)):
                    for q in range(seen + 1, part_of[c1 - 1] + 1):
                        sp.wait_ge(part_done[i][q], p + 1)
                        sp.sem_inc(sp_seen, 1)
                        seen = q
                    dst = terms[i, c0:c1].rearrange("c r n -> r c n")
                    if i == 0:
                        src = part[:, 0, part_of[c0]].unsqueeze(1).to_broadcast([P, c1 - c0, UNIT])
                    else:
                        src = part[:, 1, 0:c1 - c0]
                    sp.dma_start(dst, src).then_inc(terms_out, 16)

            def read_terms(p, u):
                sp.wait_ge(b_mm, count((p - 1) * (PAIR_TILES * FILLS)))
                sp.sem_inc(sp_seen, 1)
                sp.wait_ge(terms_out, (p + 1) * (16 * SPREAD_WRITES))
                r = QROWS // QUADS
                for j in range(QUADS):
                    for i, dst in ((1, k_dense[u][r * j:r * (j + 1)]), (0, q_bd[u][r * j:r * (j + 1), j])):
                        sp.dma_start(dst, terms[i, :, 32 * j:32 * (j + 1)]).then_inc(stacked, 16)

            def spread_max(h, u, s):
                sp.wait_ge(mT_done, h + 1)
                sp.sem_inc(sp_seen, 1)
                for j in range(QUADS):
                    sp.dma_start(q_bd[u][QROWS + PARTS * j:QROWS + PARTS * (j + 1), j, :, s * L:(s + 1) * L],
                                 mT[j * PARTS * TILES:(j + 1) * PARTS * TILES]).then_inc(m_in, 16)

            def store(p):
                p, n = sp.snap(p), sp.snap(p + 1)
                sp.wait_ge(y_ready, n)
                sp.dma_start(out_units[:, bass.ds(p, 1)], y_s[:].unsqueeze(1)).then_inc(stored, 16)

            def slots(it, last):
                for k in range(SLOTS):
                    if k in MAX_AT and not (last and MAX_AT[k] > 3):
                        g = MAX_AT[k]
                        spread_max(it * 4 + g, (g // 2) % 2, g % 2)
                    for u in range(2):
                        if last:
                            break
                        if k == Q_TERMS_AT[u]:
                            write_terms(it * 2 + 2 + u, 0)
                        if k == K_TERMS_AT[u]:
                            write_terms(it * 2 + 2 + u, 1)
                        if k == READ_AT[u] and u == 0:
                            read_terms(it * 2 + 2 + u, u)
                    if k == READ_AT[1] and not last:
                        read_terms(it * 2 + 3, 1)
                    if k == 0 and not last:
                        load_x_ln(it * 2 + 2)
                    if k == 9 and not last:
                        load_x_ln(it * 2 + 3)
                    if k == 1:
                        load_expert(it * 2 + 1, (it * 2 + 1) % EXPERTS, 1)
                    if k == 8:
                        load_x_res(it * 2)
                    if k == 21:
                        load_x_res(it * 2 + 1)
                    if k == 17 and not last:
                        load_expert(it * 2 + 2, (it * 2 + 2) % EXPERTS, 0)
                    if k == OUT_AT[0] + 3:
                        store(it * 2)
                    if k == SLOTS - 1:
                        store(it * 2 + 1)

            load_x_ln(0)
            for dst, src in wo_loads:
                sp.dma_start(dst, src).then_inc(wo_in, 16)
            load_expert(0, 0, 0)
            sp.wait_ge(cleared, 1)
            sp.wait_ge(ready_pool, 1)
            load_x_ln(1)
            for u in range(2):
                for i in range(2):
                    write_terms(u, i)
                read_terms(u, u)
            for h in range(2):
                spread_max(h, 0, h)
            with sp.Fori(0, TURNS - 1) as it:
                slots(it, False)
            slots(TURNS - 1, True)
            sp.wait_ge(stored, 16 * UNITS)

        @block.tensor
        def _(pe):
            pe.wait_ge(loaded, all_loaded)
            pe.wait_ge(ready_dve, 1)
            pe.wait_ge(ready_pool, 1)

            def prep_turn(p):
                pe.wait_ge(xh_done, p + 1)
                pe.wait_ge(v_ready, p)
                for c in range(NC):
                    t = nc.tensor.transpose(chunk(PREP, c), xh[:, c], ident[:])
                t.then_inc(x_turn, 1)

            def prep_qk(p, i):
                pe.wait_ge(hT_done, p + 1)
                if i == 1:
                    pe.wait_ge(part_left[0], p + 1)
                nc.tensor.matmul(PREP[:], wqk_p[:, i].rearrange("p j d t -> p (j d t)"), hT[:], start=True, stop=True
                                 ).then_inc(qk_mm[i], 1)

            def prep_v(p):
                pe.wait_ge(part_left[1], p + 1)
                for c in range(NC):
                    t = nc.tensor.matmul(chunk(PREP, c), chunk(hT, c), wv_s[:], start=True, stop=True)
                t.then_inc(v_mm, 1)

            def turn_max(h):
                pe.wait_ge(m_part2, h + 1)
                pe.wait_ge(mT_done, h)
                for q in range(2):
                    t = nc.tensor.matmul(chunk(PREP, q), m_part[:, q], ident_bf[:], start=True, stop=True)
                t.then_inc(m_turn, 1)

            def a_fill(it, a, f):
                u, s, t = where(a)
                n = (it * SLOTS + a) * FILLS + f
                if f == 0 and t == 0 and s == 0:
                    pe.wait_ge(stacked, (it * 2 + (a // PAIR_TILES + 1)) * (16 * SPREAD_READS))
                pe.wait_ge(a_max, count(n - 1))
                for i in range(2):
                    j = 2 * (f % 2) + i
                    q0 = s * L + (f // 2) * P
                    m = nc.tensor.matmul(A_BANK[f % 2][:, i * L:(i + 1) * L], q_bd[u][0:QROWS, j, t, q0:q0 + P],
                                         k_dense[u][0:QROWS, t, s * L:(s + 1) * L], start=True, stop=True)
                m.then_inc(a_mm, 1)

            def b_fill(it, T, f):
                u, s, t = where(T)
                n = T * FILLS + f
                if f == 0 and t == 0:
                    pe.wait_ge(m_in, (it * 4 + (T // TILES + 1)) * (16 * QUADS))
                first = FIRST * FILLS
                prev = first if first <= n < first + 3 else n - 2
                pe.wait_ge(b_exp, count(it * (SLOTS * FILLS) + prev))
                j, k0 = 2 * (f % 2), s * L + (f // 2) * P
                nc.tensor.matmul(B_BANK[b_bank(n)][:], k_dense[u][:, t, k0:k0 + P],
                                 q_bd[u][:, j:j + 2, t, s * L:(s + 1) * L], start=True, stop=True).then_inc(b_mm, 1)

            def times_v(it, T, k):
                u, s, t = where(T)
                n = it * SLOTS + T
                if k == 0 and T % 2 == 0:
                    pe.wait_ge(pv_out, it * (SLOTS // 2) + T // 2)
                if k == 0 and t == 0 and s == 0:
                    pe.wait_ge(v_ready, it * 2 + (T // PAIR_TILES + 1))
                pe.wait_ge(b_exp, n * FILLS + 2 * (k + 1))
                for j in range(QUADS):
                    m = nc.tensor.matmul(PV_BANK[32 * j:32 * j + VW, (T % 2) * L:(T % 2 + 1) * L],
                                         v_ones[u][:, 2 * s + k, QUADS * t + j], prob[T % 2][:, k, j],
                                         start=(k == 0), stop=(k == 1), skip_group_check=True)
                if k == 1:
                    m.then_inc(pv_mm, 1)

            def project(p):
                pe.wait_ge(att_done, p * 2 + 2)
                pe.wait_ge(y_sum, p)
                for c in range(NC):
                    t = nc.tensor.matmul(chunk(TAIL, c), chunk(att, c), wo_p[:], start=True, stop=True)
                t.then_inc(o_mm, 1)

            def turn_o(p):
                pe.wait_ge(o_done, p + 1)
                for c in range(NC):
                    t = nc.tensor.transpose(chunk(TAIL, c), o_s[:, c], ident[:])
                t.then_inc(o_turn, 1)

            def expert_in(p, u, f, halves):
                if f == 0:
                    pe.wait_ge(w_in, (p + 1) * (16 * W_DMAS))
                    pe.wait_ge(mT_done, halves)
                pe.wait_ge(oT_done, p + 1)
                if f >= 2:
                    pe.wait_ge(gelu, p * NF + (f - 1))
                nc.tensor.matmul((PREP, TAIL)[f % 2][:], w1_s[u][:, f * P:(f + 1) * P], oT[:], start=True, stop=True
                                 ).then_inc(f1_mm, 1)

            def expert_out(p, u):
                pe.wait_ge(gelu, (p + 1) * NF)
                for c in range(NC):
                    for f in range(NF):
                        t = nc.tensor.matmul(chunk(TAIL, c), chunk(hidden[:, f], c), w2_s[u][:, f],
                                             start=(f == 0), stop=(f == NF - 1))
                t.then_inc(f2_mm, 1)

            def slots(it, last):
                for k in range(SLOTS):
                    T, a = FIRST + k, FIRST + LEAD + k
                    for f in range(FILLS):
                        if f == 0 and k in MAX_AT and not (last and MAX_AT[k] > 3):
                            if k in (11, 27) and not last:
                                pe.wait_ge(v_ready, it * 2 + (3 if k == 11 else 4))
                            if k == 19:
                                pe.wait_ge(part_left[1], it * 2 + 4)
                            turn_max(it * 4 + MAX_AT[k])
                        for u in range(2):
                            p = it * 2 + 2 + u
                            if f == 0 and not last:
                                if k == TURN_AT[u]:
                                    pe.wait_ge(mT_done, it * 4 + (3, 4)[u])
                                    prep_turn(p)
                                if k == Q_AT[u]:
                                    prep_qk(p, 0)
                                if k == K_AT[u]:
                                    prep_qk(p, 1)
                                if k == V_AT[u]:
                                    pe.wait_ge(mT_done, it * 4 + (3, 5)[u])
                                    prep_v(p)
                            p = it * 2 + u
                            if f == 0 and k == O_AT[u]:
                                project(p)
                            if f == 0 and k == OT_AT[u]:
                                turn_o(p)
                            if k == F1_AT[u]:
                                expert_in(p, u, f, it * 4 + (4, 4 if last else 6)[u])
                        if not (last and T >= SLOTS):
                            b_fill(it, T, f)
                        if not (last and a >= SLOTS):
                            a_fill(it, a, f)
                        if f in PV_FILLS and not (last and T > SLOTS):
                            times_v(it, T - 1, PV_FILLS.index(f))
                    for u in range(2):
                        if k == F2_AT[u]:
                            expert_out(it * 2 + u, u)

            for p in range(2):
                prep_turn(p)
                prep_qk(p, 0)
                prep_qk(p, 1)
                prep_v(p)
            pe.wait_ge(wo_in, 16 * len(wo_loads))
            for T in range(-LEAD, FIRST):
                if T in (-2, 6):
                    pe.wait_ge(v_ready, 2)
                    turn_max((T + 2) // TILES)
                for f in range(FILLS):
                    if T >= 0:
                        b_fill(0, T, f)
                    a_fill(0, T + LEAD, f)
                    if f in PV_FILLS and T >= 1:
                        times_v(0, T - 1, PV_FILLS.index(f))
            with pe.Fori(0, TURNS - 1) as it:
                slots(it, False)
            slots(TURNS - 1, True)

        @block.scalar
        def _(act):
            act.wait_ge(loaded, all_loaded)
            act.wait_ge(ready_dve, 1)
            act.wait_ge(ready_pool, 1)

            def scale_hT(p):
                act.wait_ge(x_turn, p + 1)
                nc.scalar.activation(hT[:], PREP[:], ACT.Identity, scale=g_s[:, 0:1], bias=g_s[:, 1:2]
                                     ).then_inc(hT_done, 1)

            def first_part(p, i):
                if i == 0:
                    act.wait_ge(terms_out, p * (16 * SPREAD_WRITES))
                act.wait_ge(qk_mm[i], p + 1)
                nc.scalar.activation(part[:, i, 0], PREP[:], ACT.Copy).then_inc(part_done[i][0], 1)

            def second_part(p, i):
                act.wait_ge(part_left[i], p + 1)
                nc.scalar.activation(part[:, i, 1], left[:], ACT.Copy).then_inc(part_done[i][1], 1)

            def keep_v(p, u):
                act.wait_ge(v_mm, p + 1)
                act.wait_ge(pv_mm, count((p - 1) * PAIR_TILES))
                nc.scalar.activation(v_ones[u][:, :, :, 0:AE], PREP[:].rearrange("p (c h d) -> p c h d", c=NC, d=AE),
                                     ACT.Copy).then_inc(v_ready, 1)

            def keep_max(h):
                act.wait_ge(m_in, h * (16 * QUADS))
                act.wait_ge(m_turn, h + 1)
                nc.scalar.activation(mT[:], PREP[:, 0:L], ACT.Copy).then_inc(mT_done, 1)

            def exp(it, T, f):
                n = T * FILLS + f
                act.wait_ge(b_mm, it * (SLOTS * FILLS) + (n + 1))
                if f == 0:
                    act.wait_ge(pv_mm, count(it * SLOTS + (T - 1)))
                j = 2 * (f % 2)
                nc.scalar.activation(prob[T % 2][:, f // 2, j:j + 2].rearrange("p j q -> p (j q)"),
                                     B_BANK[b_bank(n)][:], ACT.Exp, scale=AE ** -0.5).then_inc(b_exp, 1)

            def keep_pv(it, T):
                t = T % TILES
                if t == 1:
                    act.wait_ge(pv_moved, count((it * 4 + (T // TILES - 1)) * (16 * 2 * QUADS)))
                act.wait_ge(pv_mm, it * SLOTS + (T + 1))
                nc.scalar.activation(pv_s[T // TILES % 2][:, t - 1:t + 1].rearrange("p t q -> p (t q)"),
                                     PV_BANK[:], ACT.Copy
                                     ).then_inc(pv_out, 1)

            def keep_oT(p):
                act.wait_ge(o_turn, p + 1)
                act.wait_ge(f1_mm, p * NF)
                nc.scalar.activation(oT[:], TAIL[:], ACT.Copy).then_inc(oT_done, 1)

            def gelus(p, u):
                act.wait_ge(f2_mm, p)
                for f in range(NF):
                    act.wait_ge(f1_mm, p * NF + (f + 1))
                    nc.scalar.activation(hidden[:, f], (PREP, TAIL)[f % 2][:], ACT.Gelu, bias=b1_s[u][:, f:f + 1]
                                         ).then_inc(gelu, 1)

            def slots(it, last):
                for k in range(SLOTS):
                    T = FIRST + k
                    if k in MAX_AT and not (last and MAX_AT[k] > 3):
                        keep_max(it * 4 + MAX_AT[k])
                    for u in range(2):
                        p = it * 2 + 2 + u
                        if not last:
                            if k == TURN_AT[u]:
                                scale_hT(p)
                            for i, at in enumerate((Q_AT, K_AT)):
                                if k == at[u]:
                                    first_part(p, i)
                            if k == V_AT[u]:
                                keep_v(p, u)
                        if k == OT_AT[u]:
                            keep_oT(it * 2 + u)
                    for f in range(FILLS):
                        if not (last and T >= SLOTS):
                            exp(it, T, f)
                        if f == GELU_FILL:
                            for u in range(2):
                                if k == F1_AT[u]:
                                    gelus(it * 2 + u, u)
                        if f == 1:
                            for u in range(2):
                                for i, at in enumerate((Q_AT, K_AT)):
                                    if k == at[u] and not last:
                                        second_part(it * 2 + 2 + u, i)
                        if f == PV_OUT_FILL and T % 2 == 0 and not (last and T > SLOTS):
                            keep_pv(it, T - 1)

            for p in range(2):
                scale_hT(p)
                for i in range(2):
                    first_part(p, i)
                    second_part(p, i)
                keep_v(p, p)
            for T in range(-LEAD, FIRST):
                if T in (-2, 6):
                    keep_max((T + 2) // TILES)
                for f in range(FILLS):
                    if T >= 0:
                        exp(0, T, f)
                    if f == PV_OUT_FILL and T >= 1 and T % 2 == 0:
                        keep_pv(0, T - 1)
            with act.Fori(0, TURNS - 1) as it:
                slots(it, False)
            slots(TURNS - 1, True)

        @block.gpsimd
        def _(pool):
            nc.gpsimd.memset(minus_half[:], -0.5)
            nc.gpsimd.memset(eps[:], EPS)
            nc.gpsimd.memset(minus_one[:], -1.0)
            nc.gpsimd.memset(zero[:], 0.0)
            nc.gpsimd.memset(m_part[:], 0.0)
            for u in range(2):
                nc.gpsimd.memset(v_ones[u][:], 1.0)
            nc.gpsimd.memset(q_bd[1][:], 0.0).then_inc(ready_pool, 1)
            pool.wait_ge(ready_pool, 1)

            def norm_root(p):
                inverse_root(nc, pool, mv, var, rstd, eps, minus_half, n_stat, n_var, n_root, p + 1)

            def third_part(p, i):
                pool.wait_ge(part_done[i][1], p + 1)
                nc.gpsimd.tensor_tensor(part[:, i, 2], left[:], part[:, i, 1], ALU.subtract
                                        ).then_inc(part_done[i][2], 1)

            def split_max(h, par):
                def parts(c):
                    return m_part[:, :, 0:PARTS * QUADS * TILES].rearrange(
                        "p q (j c t) -> p q j c t", j=QUADS, c=PARTS)[:, :, :, c]
                src = mx[par][:].rearrange("p q t j -> p q j t")
                pool.wait_ge(a_max, (h + 1) * (TILES * FILLS))
                nc.gpsimd.tensor_tensor(m_neg[:], src, minus_one[:], ALU.mult).then_inc(m_neg_done, 1)
                pool.wait_ge(m_turn, h)
                nc.gpsimd.tensor_tensor(parts(0), src, minus_one[:], ALU.mult).then_inc(m_part0, 1)
                pool.wait_ge(m_neg_done, h + 1)
                pool.wait_ge(m_part0, h + 1)
                nc.gpsimd.tensor_tensor(m_left[:], m_neg[:], parts(0), ALU.subtract).then_inc(m_left_done, 1)
                pool.wait_ge(m_left_done, h + 1)
                nc.gpsimd.tensor_tensor(parts(1), m_left[:], zero[:], ALU.add).then_inc(m_part1, 1)
                pool.wait_ge(m_part1, h + 1)
                nc.gpsimd.tensor_tensor(parts(2), m_left[:], parts(1), ALU.subtract).then_inc(m_part2, 1)

            def collect(h, s):
                pool.wait_ge(att_done, h)
                pool.sem_inc(pool_seen, 1)
                pool.wait_ge(pv_out, (h + 1) * (TILES // 2))
                pool.sem_inc(pool_seen, 1)
                for j in range(QUADS):
                    for k, dst in enumerate((att_n, att_d)):
                        pool.dma_start(dst[32 * j:32 * (j + 1), s * L:(s + 1) * L],
                                     pv_s[s][32 * j + AE * k:32 * j + AE * (k + 1)]).then_inc(pv_moved, 16)

            def add_b2(p, u):
                pool.wait_ge(x_res_in, (p + 1) * 16)
                pool.wait_ge(w_in, (p + 1) * (16 * W_DMAS))
                pool.wait_ge(y_sum, p)
                nc.gpsimd.tensor_tensor(x_b2[:], x_res[:], b2_s[u][:].unsqueeze(1).to_broadcast([P, NC, D]), ALU.add
                                        ).then_inc(x_b2_done, 1)

            def out_root(p):
                inverse_root(nc, pool, mv2, var2, rstd2, eps, minus_half, n2_stat, n2_var, n2_root, p + 1)

            def slots(it, last):
                for k in range(SLOTS):
                    if k + 1 in MAX_AT and not (last and MAX_AT[k + 1] > 3):
                        split_max(it * 4 + MAX_AT[k + 1], MAX_AT[k + 1] % 2)
                    for u in range(2):
                        if not last:
                            p = it * 2 + 2 + u
                            if k == LN_AT[u]:
                                norm_root(p)
                            for i, at in enumerate((Q_AT, K_AT)):
                                if k == at[u]:
                                    third_part(p, i)
                        if k == O_AT[u] - 1:
                            add_b2(it * 2 + u, u)
                    if k in COLLECT_AT:
                        collect(it * 4 + COLLECT_AT[k], COLLECT_AT[k] % 2)
                    for u in range(2):
                        if k == OUT_AT[u] + 1:
                            out_root(it * 2 + u)

            for p in range(2):
                norm_root(p)
                for i in range(2):
                    third_part(p, i)
            for h in range(2):
                split_max(h, h)
            with pool.Fori(0, TURNS - 1) as it:
                slots(it, False)
            slots(TURNS - 1, True)

        @block.vector
        def _(dve):
            for u in range(2):
                nc.vector.memset(k_dense[u][QROWS:P], 1.0)
            nc.vector.memset(PV_BANK[:], 0.0)
            nc.vector.memset(q_bd[0][:], 0.0).then_inc(cleared, 1)
            dve.wait_ge(loaded, all_loaded)
            nc.vector.tensor_copy(ident_bf[:], ident[:])
            for i in range(2):
                t = nc.vector.tensor_copy(wqk_p[:, i], wqk_raw[:, i].rearrange("p (t j d) -> p j d t", j=QUADS, d=AE))
            t.then_inc(ready_dve, 1)
            dve.wait_ge(ready_dve, 1)
            dve.wait_ge(ready_pool, 1)

            def norm_stats(p):
                dve.wait_ge(x_ln_in, (p + 1) * 16)
                layer_norm_stats(nc, dve, x_ln, bn, mv, n_half, n_seen, n_stat, p + 1)

            def norm_apply(p):
                dve.wait_ge(x_turn, p)
                normalise(nc, dve, x_ln, xh, mv, rstd, n_root, p + 1, xh_done)

            def take_first_part(p, i):
                if i == 0:
                    dve.wait_ge(part_done[1][2], p)
                else:
                    dve.wait_ge(part_done[0][2], p + 1)
                dve.wait_ge(part_done[i][0], p + 1)
                nc.vector.tensor_tensor(left[:], PREP[:], part[:, i, 0], ALU.subtract).then_inc(part_left[i], 1)

            def maxima(it, a, f):
                u, s, t = where(a)
                n = (it * SLOTS + a) * FILLS + f
                if t == 0 and f == 0:
                    dve.wait_ge(m_left_done, count(it * 4 + (a // TILES - 1)))
                dve.wait_ge(a_mm, n + 1)
                q, j = f // 2, 2 * (f % 2)
                nc.vector.tensor_reduce(mx[s][:, q, t, j:j + 2], A_BANK[f % 2][:].rearrange("p (j k) -> p j k", j=2),
                                        AX.X, ALU.max).then_inc(a_max, 1)

            def attend_half(it, g):
                s, h, p = g % 2, it * 4 + g, it * 2 + g // 2
                c = slice(s * L, (s + 1) * L)
                dve.wait_ge(pv_moved, (h + 1) * (16 * 2 * QUADS))
                nc.vector.reciprocal(att_d[:, c], att_d[:, c]).then_inc(sums_inv, 1)
                dve.wait_ge(sums_inv, h + 1)
                dve.wait_ge(o_mm, p)
                nc.vector.tensor_tensor(att[:, c], att_n[:, c], att_d[:, c], ALU.mult).then_inc(att_done, 1)

            def add_residual(p):
                dve.wait_ge(o_mm, p + 1)
                dve.wait_ge(x_res_in, (p + 1) * 16)
                dve.wait_ge(o_turn, p)
                nc.vector.tensor_tensor(flat(o_s), TAIL[:], flat(x_res), ALU.add).then_inc(o_done, 1)

            def add_expert(p):
                dve.wait_ge(f2_mm, p + 1)
                dve.wait_ge(x_b2_done, p + 1)
                dve.wait_ge(stored, p * 16)
                nc.vector.tensor_tensor(flat(y_s), TAIL[:], flat(x_b2), ALU.add).then_inc(y_sum, 1)

            def out_stats(p):
                dve.wait_ge(y_sum, p + 1)
                layer_norm_stats(nc, dve, y_s, bn2, mv2, n2_half, n2_seen, n2_stat, p + 1)

            def finish(p):
                normalise(nc, dve, y_s, y_s, mv2, rstd2, n2_root, p + 1, y_ready)

            def slots(it, last):
                for k in range(SLOTS):
                    a = FIRST + LEAD + k
                    for f in range(FILLS):
                        if not (last and a >= SLOTS):
                            maxima(it, a, f)
                        for u in range(2):
                            p = it * 2 + 2 + u
                            if not last:
                                if (k, f) == (LN_AT[u], 0):
                                    norm_stats(p)
                                if (k, f) == (LN_AT[u] + 1, 2):
                                    norm_apply(p)
                                for i, at in enumerate((Q_AT, K_AT)):
                                    if (k, f) == (at[u], 0):
                                        take_first_part(p, i)
                            p = it * 2 + u
                            if (k, f) == (ATTEND_AT[u], 0):
                                attend_half(it, 2 * u + 1)
                            if (k, f) == (EVEN_AT[u], 0):
                                attend_half(it, 2 * u)
                            if (k, f) == (O_AT[u], 0):
                                add_residual(p)
                            if (k, f) == (OUT_AT[u], 0):
                                add_expert(p)
                            if (k, f) == (OUT_AT[u], 3):
                                out_stats(p)
                            if (k, f) == (OUT_AT[u] + 1, 3):
                                finish(p)

            for p in range(2):
                norm_stats(p)
                norm_apply(p)
                for i in range(2):
                    take_first_part(p, i)
            for T in range(-LEAD, FIRST):
                for f in range(FILLS):
                    maxima(0, T + LEAD, f)
            with dve.Fori(0, TURNS - 1) as it:
                slots(it, False)
            slots(TURNS - 1, True)


def build(nc, out, attn_in, ffn_in, c_xpos, c_mask, c_ident):
    with ExitStack() as ctx:
        bank = [ctx.enter_context(nc.psum_tensor(f"bank{i}", [P, 512], F32)) for i in range(8)]
        x1_all = ctx.enter_context(nc.sbuf_tensor("x1_all", [P, UNITS, NC, D], F32))
        used = retention_block(nc, bank, x1_all, *attn_in, c_xpos, c_mask, c_ident)
        nc.clear_and_free_semaphores(used)
        nc.all_engine_barrier()
        terms = nc.dram_tensor("terms", [2, TERMS, P, UNIT], BF16, kind="Internal").ap()
        attention_block(nc, bank, x1_all, terms, out, *ffn_in, c_ident)


def constants():
    import numpy as np

    pos = np.arange(L, dtype=np.float32)
    base = ((np.arange(0, RE, 2, dtype=np.float32) + np.float32(0.4 * RE)) / np.float32(1.4 * RE)).astype(np.float64)
    scale = base[None, :] ** (pos / np.float32(512.0)).astype(np.float64)[:, None]
    half = RE // 2
    inv = (1.0 / 10000.0 ** (np.arange(half) / half)).astype(np.float32)
    angle = (pos[:, None] * inv[None, :]).astype(np.float32).astype(np.float64)
    gamma = (1.0 - np.exp(np.linspace(np.log(1 / 32), np.log(1 / 64), RH))).astype(np.float32)
    log_gamma = np.log(gamma).astype(np.float32).astype(np.float64)
    decay = np.exp(log_gamma[:, None] * (np.arange(L) - L // 2)[None, :])
    out = np.zeros((4, RE, RH, L))
    for i, (s, dec) in enumerate(((scale, decay), (1.0 / scale, 1.0 / decay))):
        for e in range(RE):
            out[2 * i, e] = (np.cos(angle) * s)[:, e // 2][None, :] * dec
            out[2 * i + 1, e] = (np.sin(angle) * s)[:, e // 2][None, :] * dec
    xpos = out.reshape(4, P, L).transpose(1, 0, 2).astype(np.float32)
    mask = (np.arange(P)[:, None] <= np.arange(P)[None, :]).astype(np.float32)
    return {"c_xpos": np.ascontiguousarray(xpos), "c_mask": mask, "c_ident": np.eye(P, dtype=np.float32)}


_A = ["X", "Wq", "Wk", "Wv", "W_G", "W_O", "gn_w", "gn_b", "ln1_w", "ln1_b", "ln2_w", "ln2_b",
      "ffn_w1", "ffn_b1", "ffn_w2", "ffn_b2"]
_F = ["ln_g", "ln_b", "wq", "wk", "wv", "wo", "w1", "b1", "w2", "b2"]


def kernel(**inputs):
    import numpy as _np
    import concourse.bacc as _bacc
    from concourse.bass_utils import run_bass_kernel_spmd as _run
    nc = _bacc.Bacc("TRN2", target_bir_lowering=False, num_devices=1)
    arrays, args = {}, {}
    for name in ["L0_attn_" + s for s in _A] + ["L0_ffn_" + s for s in _F]:
        arrays[f"in_{name}"] = _np.ascontiguousarray(inputs[name])
    arrays.update(constants())
    for k, v in arrays.items():
        args[k] = nc.dram_tensor(k, v.shape, mybir.dt.from_np(v.dtype), kind="ExternalInput").ap()
    out = nc.dram_tensor("out_0_dram", (SEQS, L, D), F32, kind="ExternalOutput").ap()
    build(nc, out, [args[f"in_L0_attn_{s}"] for s in _A], [args[f"in_L0_ffn_{s}"] for s in _F],
          args["c_xpos"], args["c_mask"], args["c_ident"])
    r = _run(nc, [arrays], core_ids=[0])
    return r.results[0]["out_0_dram"]
```
